# Optimizing a Trainium2 kernel written in Bass

```python
import numpy as np
import jax
import jax.numpy as jnp

def _softmax(x, axis=-1):
    return jax.nn.softmax(x, axis=axis)
def _gelu(x):
    return jax.nn.gelu(x, approximate=True)
def _silu(x):
    return jax.nn.silu(x)
def _sigmoid(x):
    return jax.nn.sigmoid(x)
def _layernorm(x, axis=-1, eps=1e-5):
    m = jnp.mean(x, axis=axis, keepdims=True)
    v = jnp.var(x, axis=axis, keepdims=True)
    return (x - m) / jnp.sqrt(v + eps)
def _scatter_add(tgt, idx, src, axis=0):
    return tgt.at[idx].add(src)
def _segment_sum(src, seg, n):
    return jax.ops.segment_sum(src, seg, n)

kernel_name = 'mk_conv_preact_d2_conv_nchw16_cb7268'

def setup_inputs(seed: int = 0):
    np.random.seed(seed)
    _w = jnp.asarray
    def _rec_inputs():
        import jax
        import jax.numpy as jnp
        _gk = jax.random.key(seed)
        x = -0.0001546 + 1 * jax.random.normal(jax.random.fold_in(_gk, 1), (1, 16, 2048, 2048), jnp.float32)
        return x
    x = _rec_inputs()
    def _L0_conv_setup():
        import jax, jax.numpy as jnp
        import numpy as np
        N, C, H, W = (2, 16, 2048, 2048)
        R, S = (6, 11)
        PAD_H, PAD_W = (5, 5)
        key = jax.random.key(seed)
        k1, k2 = jax.random.split(key)
        x = jax.random.normal(k1, (N, C, H, W), dtype=jnp.float32)
        weight = jax.random.normal(k2, (C, R, S), dtype=jnp.float32) * 0.1
        return {'x': x, 'weight': weight}
    _L0_conv_all = _L0_conv_setup()
    _L0_conv_in = {k: v for k, v in _L0_conv_all.items() if k in ('weight', )}
    del _L0_conv_all

    def _L1_conv_setup():
        import jax, jax.numpy as jnp
        import numpy as np
        key = jax.random.key(seed)
        ks = jax.random.split(key, 7)
        B, H, N = (2, 16, 2048)
        DIM = 64
        qk_dots = jax.random.normal(ks[0], (B, H, N, N), dtype=jnp.float32)
        W1 = jax.random.normal(ks[1], (1, DIM), dtype=jnp.float32) / 1.0
        b1 = jnp.zeros((DIM,), dtype=jnp.float32)
        W2 = jax.random.normal(ks[2], (DIM, DIM), dtype=jnp.float32) / np.sqrt(DIM)
        b2 = jnp.zeros((DIM,), dtype=jnp.float32)
        W3 = jax.random.normal(ks[3], (DIM, H), dtype=jnp.float32) / np.sqrt(DIM)
        b3 = jnp.zeros((H,), dtype=jnp.float32)
        return {'qk_dots': qk_dots, 'W1': W1, 'b1': b1, 'W2': W2, 'b2': b2, 'W3': W3, 'b3': b3}
    _L1_conv_all = _L1_conv_setup()
    _L1_conv_in = {k: v for k, v in _L1_conv_all.items() if k in ('W1', 'b1', 'W2', 'b2', 'W3', 'b3', )}
    del _L1_conv_all

    return {
        "x": x,
        "L0_conv_weight": _L0_conv_in["weight"],
        "L1_conv_W1": _L1_conv_in["W1"],
        "L1_conv_b1": _L1_conv_in["b1"],
        "L1_conv_W2": _L1_conv_in["W2"],
        "L1_conv_b2": _L1_conv_in["b2"],
        "L1_conv_W3": _L1_conv_in["W3"],
        "L1_conv_b3": _L1_conv_in["b3"],
    }

def reference(x, L0_conv_weight, L1_conv_W1, L1_conv_b1, L1_conv_W2, L1_conv_b2, L1_conv_W3, L1_conv_b3):
    import jax
    import jax.numpy as jnp
    def _L0_conv_ref(x, weight):
        import jax, jax.numpy as jnp
        import numpy as np
        N, C, H, W = (2, 16, 2048, 2048)
        R, S = (6, 11)
        PAD_H, PAD_W = (5, 5)
        causal_mask = jnp.tril(jnp.ones((H, W), dtype=bool))
        xm = jnp.where(causal_mask, x, jnp.zeros((), x.dtype))
        y = jax.lax.conv_general_dilated(xm, weight[:, None, :, :], window_strides=(1, 1), padding=((PAD_H, R - 1 - PAD_H), (PAD_W, S - 1 - PAD_W)), dimension_numbers=('NCHW', 'OIHW', 'NCHW'), feature_group_count=C)
        return jnp.where(causal_mask, y, jnp.zeros((), y.dtype))

    def _L1_conv_ref(qk_dots, W1, b1, W2, b2, W3, b3):
        import jax, jax.numpy as jnp
        import numpy as np
        n = qk_dots.shape[-1]
        dtype = qk_dots.dtype
        pos = jnp.arange(-n + 1, n, dtype=dtype)[:, None]
        h = jax.nn.relu(pos @ W1 + b1)
        h = jax.nn.relu(h @ W2 + b2)
        table = h @ W3 + b3
        idx = jnp.arange(n)[:, None] - jnp.arange(n)[None, :] + (n - 1)
        bias = table[idx]
        bias = jnp.transpose(bias, (2, 0, 1))
        return qk_dots + bias

    def _gn(v, G=8, eps=1e-5):
        B_, C_, H_, W_ = v.shape
        g = v.reshape(B_, G, C_ // G, H_, W_)
        m = jnp.mean(g, axis=(2, 3, 4), keepdims=True)
        s = jnp.var(g, axis=(2, 3, 4), keepdims=True)
        return ((g - m) / jnp.sqrt(s + eps)).reshape(v.shape)

    def _ln_c(v, eps=1e-6):
        m = jnp.mean(v, axis=1, keepdims=True)
        s = jnp.var(v, axis=1, keepdims=True)
        return (v - m) / jnp.sqrt(s + eps)

    def _ln_t(v, eps=1e-5):
        m = jnp.mean(v, axis=-1, keepdims=True)
        s = jnp.var(v, axis=-1, keepdims=True)
        return (v - m) / jnp.sqrt(s + eps)

    def _to_tokens(v):
        B_, C_, H_, W_ = v.shape
        return v.reshape(B_, C_, H_ * W_).transpose(0, 2, 1)
    def _from_tokens(t, like):
        B_, C_, H_, W_ = like.shape
        return t.transpose(0, 2, 1).reshape(B_, C_, H_, W_)

    x = x + _L0_conv_ref(_gn(x), L0_conv_weight)
    x = x + _L1_conv_ref(_gn(x), L1_conv_W1, L1_conv_b1, L1_conv_W2, L1_conv_b2, L1_conv_W3, L1_conv_b3)
    return x


_drawn_inputs = setup_inputs


def setup_inputs(seed=0):
    import zlib

    import numpy as np

    out = dict(_drawn_inputs(seed))
    spreads = {'L1_conv_b1': (0.0, 2.0), 'L1_conv_b2': (0.0, 2.0), 'L1_conv_b3': (0.0, 2.0)}
    factors = {'x': 8.0, 'L0_conv_weight': 38.509}
    for name, (base, spread) in spreads.items():
        noise = np.random.default_rng([zlib.crc32(name.encode()), seed]).standard_normal(out[name].shape)
        drawn = base * np.exp(spread * noise) if base else spread * noise
        out[name] = jnp.asarray(drawn.astype(out[name].dtype))
    for name, factor in factors.items():
        out[name] = (out[name] * factor).astype(out[name].dtype)
    return out
```

```python
import concourse.bass as bass
from concourse import mybir
from contextlib import ExitStack


def preact_conv_kernel(nc, x, wflip, w1, b1, w2, b2, w3, b3, out):
    f32, f16, bf16 = mybir.dt.float32, mybir.dt.float16, mybir.dt.bfloat16
    ALU = mybir.AluOpType
    ACT = mybir.ActivationFunctionType
    AX = mybir.AxisListType
    RED = bass.bass_isa.ReduceOp

    _, CH, HH, WW = x.shape
    _, TR, TS = wflip.shape
    DIM = w2.shape[0]
    P, K, BW = 128, 4, 512
    CPG = 2
    G = CH // CPG
    NBAND = HH // (P * K)
    XC = P // K
    NPC = 4
    TIN = NPC * XC
    PADC = TS // 2
    TOUT = TIN - PADC
    STEP = TIN - 2 * PADC
    WC = XC + TS - 1
    NE = TR + K - 1
    ROWN = P * CPG * HH * WW // P
    NPP = ROWN // P
    EPS = 1e-5
    WSCALE = 256.0
    NB3 = 3

    def band_tiles(b):
        return -(-(BW * (b + 1) - TOUT) // STEP) + 1
    TILES = [(c, b, t) for c in range(CPG) for b in range(NBAND) for t in range(band_tiles(b))]
    NT = len(TILES)
    NTC = NT // CPG
    MAXT = band_tiles(NBAND - 1)
    is_diag = [STEP * t + TIN > BW * b for c, b, t in TILES]
    DIAG_BEFORE = [sum(is_diag[:n]) for n in range(NT + 1)]
    ND = DIAG_BEFORE[NT]

    EDGES = [(n, BW * (b + 1) - STEP * (t + 1)) for n, (c, b, t) in enumerate(TILES)
             if b < NBAND - 1 and t == band_tiles(b) - 1 and BW * (b + 1) > STEP * (t + 1)]
    assert all(w <= XC - STEP % XC for _, w in EDGES)
    edges_before = lambda n: sum(e < n for e, _ in EDGES)
    NEDGE = len(EDGES)

    LOWER = [(c, b, q) for c in range(CPG) for b in range(NBAND) for q in range(b + 1)]
    NL = len(LOWER)
    first_tile = {blk: next(n for n, (c, b, t) in enumerate(TILES)
                            if (c, b) == blk[:2] and STEP * t + TIN > BW * blk[2]) for blk in LOWER}
    last_tile = {blk: next(n for n, (c, b, t) in enumerate(TILES)
                           if (c, b) == blk[:2] and STEP * t + TOUT >= BW * (blk[2] + 1)) for blk in LOWER}
    KEPT = [blk for blk in LOWER if blk[1] >= 2]
    STREAM = [(c, b, q) for c in range(CPG) for b in range(NBAND) for q in range(NBAND)
              if (c, b, q) not in KEPT]
    NU = 2 * len(STREAM)
    NR = 2 * len(KEPT)
    NA = CPG * NBAND * NBAND * 2
    NAB, NUB = 4, 4
    UPPER_PER_CH = NBAND * (NBAND - 1) // 2
    LO_ENTRIES = CPG * (NBAND * NBAND - UPPER_PER_CH) * K

    a_pos = [3 + a * 78 // NA for a in range(NA)]
    a_load_pos = [0 if a < NAB else a_pos[a - NAB] + 1 for a in range(NA)]
    kept_pos = {}
    for blk in KEPT:
        at = max(4, first_tile[blk] - 10)
        kept_pos[blk] = (at, at + 1)
    U_SPAN = [(4, 38), (49, 38)]
    u_pos = [U_SPAN[c][0] + i * U_SPAN[c][1] // (NU // 2) for c in range(CPG) for i in range(NU // 2)]
    u_load_pos = [(0 if c == 0 else U_SPAN[c][0] - 8) if i < NUB else u_pos[c * NU // 2 + i - NUB] + 3
                  for c in range(CPG) for i in range(NU // 2)]
    u_load_pos = [max(u_load_pos[i], u_pos[i - NUB] + 3 if i >= NUB else 0) for i in range(NU)]
    BIAS_LOAD, BIAS_SHIFT = {1: 44}, {0: 3, 1: 47}
    NEXT_BIAS_LOAD, NEXT_TRANSIT_LOAD, TRANSIT1_LOAD = 88, 78, 30
    W_LOAD, W_BUILD = {1: 10, 0: 55}, {1: 20, 0: 65}
    STATS1, HAND_OVER_NORM, HAND_OVER_SUMS = (81, 82, 83, 84), 88, 5

    pieces, at, used = [], 0, 0
    for i, blk in enumerate(LOWER):
        for j in range(K + 2):
            ready = last_tile[blk] + 2
            if ready > at:
                at, used = ready, 0
            elif used == 2:
                at, used = at + 1, 0
            used += 1
            pieces.append((at, i, j))
    NPIECE = len(pieces)
    piece_end = {i: (K + 2) * (i + 1) for i in range(NL)}
    spill_pos = {i: max(a for a, ii, _ in pieces if ii == i) + 1 for i in range(NL) if LOWER[i][1] < 2}

    xv = x.rearrange("o c (b p k) w -> (o c) b p k w", p=P, k=K)
    ov = out.rearrange("o c (b p k) w -> (o c) b p k w", p=P, k=K)
    taps_dram = nc.dram_tensor("taps_scratch", [CH * TR, XC * WC], f32, kind="Internal").ap()
    taps_v = taps_dram.rearrange("(c r) (p j) -> c p r j", r=TR, j=WC)
    NPOS = 2 * HH
    bias_dram = nc.dram_tensor("bias_scratch", [CH, NPOS], f32, kind="Internal").ap()
    VLO = -(WW - 1)
    NV = BW * (NBAND - 1) + K - 1 - VLO + 1

    ctx = ExitStack()
    with ctx:
        def sb(name, shape, dt):
            return ctx.enter_context(nc.sbuf_tensor(name, shape, dt))

        def sem(name):
            return ctx.enter_context(nc.semaphore(name))

        transit = {b: sb(f"band{b}", [P, K, BW * (b + 1)], f32) for b in (0, 1)}
        kept = {(c, b): sb(f"kept_c{c}_band{b}", [P, K, BW * (b + 1)], f32)
                for c in range(CPG) for b in (2, 3)}

        def slot(c, b):
            return transit[b] if b < 2 else kept[(c, b)]

        bias = sb("bias", [P, NV], f32)
        abuf = sb("abuf", [P, NAB, 2, BW], f32)
        ubuf = sb("ubuf", [P, NUB, 2, BW], f32)
        xn = sb("xn", [P, NB3, NPC, K, XC], f32)
        XT = sb("XT", [P, NB3, 2, NPC, P + 2], f16)
        halo = sb("halo", [P, MAXT, 2, NPC, 2], f16)
        wstage = sb("wstage", [P, NE, WC], f32)
        wsplit = sb("wsplit", [P, CPG, 2, NE, WC], f16)
        MLO = BW * 0 - STEP * (band_tiles(0) - 1) - (TIN - 1)
        MW = 728
        mask = sb("mask", [P, MW], bf16)
        ident = sb("ident", [P, P], f32)
        entries = sb("entries", [P, NA * 2, 6], f32)
        nxt = sb("nxt", [P, 3], f32)
        normp = sb("normp", [P, 2], f32)
        cur = sb("cur", [P, 4], f32)
        outp = sb("outp", [P, 3], f32)
        wback = sb("wback", [P, CPG], f32)

        def col(t, i):
            return t[:, i:i + 1]
        wsc = sb("wsc", [P, CH, 2], f32)
        sums = sb("sums", [P, 2 * NL], f32)
        squares = sb("squares", [P, K * NL], f32)
        t1 = sb("t1", [P, 16], f32)
        t2 = sb("t2", [P, 16], f32)
        small = sb("small", [DIM, 8], f32)
        w2s = sb("w2s", [DIM, DIM], f32)
        w3s = sb("w3s", [DIM, CH], f32)
        psT = [ctx.enter_context(nc.psum_tensor(f"psT{i}", [P, NPC, P], f32)) for i in range(NB3)]
        psY = [ctx.enter_context(nc.psum_tensor(f"psY{i}", [P, K, TIN], f32)) for i in range(NB3)]
        junk = ctx.enter_context(nc.psum_tensor("junk", [P, BW], f32))

        def flat(t):
            return t[:, :, :].rearrange("p a b -> p (a b)")
        pos_in = flat(kept[(0, 3)])[0:DIM, 0:NPOS]
        h1 = flat(kept[(0, 3)])[0:DIM, NPOS:2 * NPOS]
        h2 = flat(kept[(1, 3)])[0:DIM, 0:NPOS]
        table = flat(kept[(1, 3)])[0:CH, NPOS:2 * NPOS]
        zeros = flat(kept[(0, 2)])[0:CH * TR, 0:XC * WC]
        wall = flat(kept[(1, 2)])[:, 0:CH * TR * TS]

        const_ready = sem("const_ready")
        small_loaded = sem("small_loaded")
        wall_loaded = sem("wall_loaded")
        zeros_ready = sem("zeros_ready")
        taps_zeroed = sem("taps_zeroed")
        taps_stored = sem("taps_stored")
        pos_ready = sem("pos_ready")
        h1_ready = sem("h1_ready")
        mlp2_done = sem("mlp2_done")
        h2_ready = sem("h2_ready")
        mlp3_done = sem("mlp3_done")
        table_ready = sem("table_ready")
        table_stored = sem("table_stored")
        scale_chain = sem("scale_chain")
        a_loaded = [sem(f"a_loaded{i}") for i in range(NAB)]
        a_done = sem("a_done")
        x_loaded = {}
        for c, b, q in LOWER:
            x_loaded[(c, b, q)] = sem(f"x_loaded_{c}{b}{q}") if b >= 2 or c == 0 else x_loaded[(0, b, q)]
        x1_spilled = {(b, q): sem(f"x1_spilled_{b}{q}") for b in (0, 1) for q in range(b + 1)}
        kept_stored = {blk: sem("kept_stored_%d%d%d" % blk) for blk in KEPT}
        u_loaded = [sem(f"u_loaded{i}") for i in range(NUB)]
        u_scaled = sem("u_scaled")
        u_added = sem("u_added")
        u_stored = [sem(f"u_stored{i}") for i in range(NUB)]
        kept_done = sem("kept_done")
        bias_loaded = sem("bias_loaded")
        bias_shifted = sem("bias_shifted")
        w_loaded = sem("w_loaded")
        w_built = sem("w_built")
        w_hi_built = sem("w_hi_built")
        wback_ready = sem("wback_ready")
        diag_normed = sem("diag_normed")
        xn_ready = sem("xn_ready")
        transposed = sem("transposed")
        hi_ready = sem("hi_ready")
        lo_ready = sem("lo_ready")
        halo_zeroed = sem("halo_zeroed")
        halo_in = sem("halo_in")
        halo_out = sem("halo_out")
        edge_copied = sem("edge_copied")
        convolved = sem("convolved")
        conv_masked = sem("conv_masked")
        evicted = sem("evicted")
        pieces_done = sem("pieces_done")
        sums_read = sem("sums_read")
        s1_chain = sem("s1_chain")
        s1_pool = sem("s1_pool")
        s1_root = sem("s1_root")
        s2_chain = sem("s2_chain")
        s2_pool = sem("s2_pool")
        s2_root = sem("s2_root")
        gn1_ready = sem("gn1_ready")
        cur_ready = sem("cur_ready")
        gn2_ready = sem("gn2_ready")

        def chan(g, c):
            return CPG * g + c

        def wait(eng, s, value):
            if not isinstance(value, int) or value > 0:
                eng.wait_ge(s, value)

        def wait_alone(eng, s, value):
            if not isinstance(value, int) or value > 0:
                eng.wait_ge(s, value)
                eng.nop(nofuse=True)

        def bias_at(b, q, h):
            start = 2 * h + BW * b - BW * q - VLO
            full = bias[:, :]
            return bass.AP(full.tensor, start, [[full.ap[0][0], P], [1, 2], [-1, BW]])

        def mask_at(b, t, c0, c1):
            start = BW * b - STEP * t - c0 - MLO
            full = mask[:, :]
            return bass.AP(full.tensor, start, [[full.ap[0][0], P], [1, K], [-1, c1 - c0]])

        block = ctx.enter_context(nc.Block())

        def stages(eng, stage):
            stage(0, True, False, False)
            stage(1, True, True, False)
            with eng.Fori(2, G) as s:
                stage(s, True, True, True)
            stage(G, False, True, True)
            stage(G + 1, False, False, True)

        def a_half(a):
            c, r = divmod(a, NBAND * NBAND * 2)
            b, r = divmod(r, NBAND * 2)
            return (c, b) + divmod(r, 2)

        @block.sync
        def _(sp):
            sp.dma_start(small[:, 0:1], w1.rearrange("o d -> d o")).then_inc(small_loaded, 16)
            sp.dma_start(small[:, 1:2], b1.rearrange("(d o) -> d o", o=1)).then_inc(small_loaded, 16)
            sp.dma_start(small[:, 2:3], b2.rearrange("(d o) -> d o", o=1)).then_inc(small_loaded, 16)
            sp.dma_start(small[0:CH, 3:4], b3.rearrange("(d o) -> d o", o=1)).then_inc(small_loaded, 16)
            sp.dma_start(w2s[:, :], w2).then_inc(small_loaded, 16)
            sp.dma_start(w3s[:, :], w3).then_inc(small_loaded, 16)
            wf = wflip.rearrange("c r s -> (c r s)")
            sp.dma_start(wall, wf.partition_broadcast(P)).then_inc(wall_loaded, 16)
            sp.wait_ge(zeros_ready, 1)
            sp.dma_start(taps_dram[:, :], zeros).then_inc(taps_zeroed, 16)
            sp.wait_ge(taps_zeroed, 16)
            sp.dma_start(bass.AP(taps_dram.tensor, 0, [[XC * WC, CH * TR], [WC + 1, XC], [1, TS]]),
                         bass.AP(wflip.tensor, 0, [[TS, CH * TR], [0, XC], [1, TS]])).then_inc(taps_stored, 16)

            def stage(s, do_a, do_b, do_c):
                ga, gb, gc = s, s - 1, s - 2
                if isinstance(s, int) and s == 1:
                    sp.wait_ge(table_ready, 8)
                    sp.dma_start(bias_dram[:, :], table).then_inc(table_stored, 16)
                    sp.wait_ge(table_stored, 16)
                    sp.wait_ge(scale_chain, 7)
                for n in range(NT):
                    if do_a:
                        for a in range(NA):
                            if a_load_pos[a] == n:
                                c, b, q, h = a_half(a)
                                wait(sp, a_done, ga * NA + a - NAB + 1)
                                sp.dma_start(abuf[:, a % NAB, :, :],
                                             xv[chan(ga, c), b][:, 2 * h:2 * h + 2, BW * q:BW * (q + 1)]
                                             ).then_inc(a_loaded[a % NAB], 16)
                    if do_b:
                        if n == TRANSIT1_LOAD:
                            load_transit(gb, 1)
                        for blk in KEPT:
                            if kept_pos[blk][1] + 3 == n:
                                c, b, q = blk
                                wait(sp, kept_stored[blk], 16 * gb)
                                sp.dma_start(kept[(c, b)][:, :, BW * q:BW * (q + 1)],
                                             xv[chan(gb, c), b][:, :, BW * q:BW * (q + 1)]
                                             ).then_inc(x_loaded[blk], 16)
                        if n == W_LOAD[1]:
                            load_taps(gb, 1)
                    if do_a and n == W_LOAD[0]:
                        load_taps(ga, 0)
                    if do_a and n == NEXT_TRANSIT_LOAD:
                        load_transit(ga, 0)
                    if do_c:
                        for u in range(NU):
                            if u_load_pos[u] == n:
                                (c, b, q), h = STREAM[u // 2], u % 2
                                wait(sp, u_stored[u % NUB], 16 * (gc * (NU // NUB) + u // NUB))
                                spilled = q <= b
                                if spilled:
                                    sp.wait_ge(x1_spilled[(b, q)], 16 * (chan(gc, c) + 1))
                                src = (ov if spilled else xv)[chan(gc, c), b]
                                sp.dma_start(ubuf[:, u % NUB, :, :], src[:, 2 * h:2 * h + 2, BW * q:BW * (q + 1)]
                                             ).then_inc(u_loaded[u % NUB], 16)
                        if n == BIAS_LOAD[1]:
                            load_bias(gc, 1)
                    if do_b and n == NEXT_BIAS_LOAD:
                        load_bias(gb, 0)

            def load_transit(g, c):
                for b in (0, 1):
                    for q in range(b + 1):
                        wait(sp, x1_spilled[(b, q)], 16 * chan(g, c))
                        sp.dma_start(transit[b][:, :, BW * q:BW * (q + 1)],
                                     xv[chan(g, c), b][:, :, BW * q:BW * (q + 1)]
                                     ).then_inc(x_loaded[(c, b, q)], 16)

            def load_taps(g, c):
                sp.wait_ge(taps_stored, 16)
                wait(sp, w_built, chan(g, c))
                if isinstance(g, int) and g == 0 and c == 0:
                    sp.wait_ge(const_ready, 6)
                for k in range(K):
                    sp.dma_start(wstage[XC * k:XC * (k + 1), k:k + TR, :], taps_v[chan(g, c)]
                                 ).then_inc(w_loaded, 16)

            def load_bias(g, c):
                wait_alone(sp, kept_done, g * NR + c * (NR // 2))
                wait(sp, u_added, g * NU + c * (NU // 2))
                row = bias_dram[bass.ds(chan(g, c), 1), :]
                src = bass.AP(row.tensor, row.offset, [[K, P], [1, NV]])
                sp.dma_start(bias[:, :], src).then_inc(bias_loaded, 16)

            stages(sp, stage)

        @block.scalar
        def _(act):
            act.wait_ge(small_loaded, 96)
            act.wait_ge(pos_ready, 1)
            act.wait_ge(const_ready, 6)
            nc.scalar.activation(h1, pos_in, ACT.Relu, bias=small[:, 1:2], scale=small[:, 0:1]).then_inc(h1_ready, 1)
            for j in range(NPOS // BW):
                cols = slice(j * BW, (j + 1) * BW)
                act.wait_ge(mlp2_done, j + 1)
                nc.scalar.activation(h2[:, cols], psT[j % 2][0:DIM, :, :].rearrange("p a b -> p (a b)"),
                                     ACT.Relu, bias=small[:, 2:3]).then_inc(h2_ready, 1)
                act.wait_ge(mlp3_done, j + 1)
                nc.scalar.activation(table[:, cols], psY[j % 2][0:CH, :, :].rearrange("p a b -> p (a b)"),
                                     ACT.Identity, bias=small[0:CH, 3:4]).then_inc(table_ready, 1)

            def norm(g, n):
                c, b, t = TILES[n]
                N = NT * g + n
                for q in range(b + 1):
                    if first_tile[(c, b, q)] == n:
                        act.wait_ge(x_loaded[(c, b, q)], 16 * (g + 1) if b >= 2 else 16 * (chan(g, c) + 1))
                wait(act, transposed, N - NB3 + 1)
                if n > 0 and is_diag[n - 1] and not is_diag[n]:
                    act.wait_ge(xn_ready, N)
                elif n == 0:
                    wait(act, xn_ready, N)
                width = min(TIN, BW * (b + 1) - STEP * t)
                whole, rest = divmod(width, XC)
                to = xn[:, n % NB3, :, :, :].rearrange("p i k c -> p k i c")
                x0 = STEP * t
                last = nc.scalar.activation(to[:, :, 0:whole, :], slot(c, b)[:, :, x0:x0 + XC * whole].rearrange(
                    "p k (i c) -> p k i c", c=XC), ACT.Identity, bias=col(normp, 1), scale=col(normp, 0))
                if rest:
                    last = nc.scalar.activation(to[:, :, whole, 0:rest], slot(c, b)[:, :, x0 + XC * whole:x0 + width],
                                                ACT.Identity, bias=col(normp, 1), scale=col(normp, 0))
                last.then_inc(diag_normed if is_diag[n] else xn_ready, 1)

            def split_hi(g, n):
                N = NT * g + n
                act.wait_ge(transposed, N + 1)
                wait(act, convolved, N - NB3 + 1)
                wait(act, halo_out, N - NB3 + 1)
                for e, _ in EDGES:
                    if n == e + NB3:
                        act.wait_ge(edge_copied, 16 * K * (NEDGE * g + edges_before(n)))
                nc.scalar.copy(XT[:, n % NB3, 0, :, 2:P + 2], psT[n % NB3][:, :, :]).then_inc(hi_ready, 1)

            def copy_edge(g, n, w):
                c, b, t = TILES[n]
                act.wait_ge(lo_ready, NT * g + n + 1)
                act.wait_ge(halo_zeroed, chan(g, c) + 1)
                piece_i, col = divmod(STEP, XC)
                for k in range(K):
                    act.dma_start(halo[XC * k:XC * k + w, t + 1, :, 0, :],
                                  XT[XC * k + col:XC * k + col + w, n % NB3, :, piece_i, P:P + 2]
                                  ).then_inc(edge_copied, 16)

            def piece(g, i, j):
                c, b, q = LOWER[i]
                if j == 0:
                    act.wait_ge(evicted, NT * g + last_tile[LOWER[i]] + 1)
                    if i == 0:
                        act.wait_ge(cur_ready, 2 * g + 2)
                        wait(act, sums_read, g)
                wait(act, pieces_done, NPIECE * g + (K + 2) * i + j)
                src = slot(c, b)
                if j < K:
                    nc.scalar.activation(junk[:, :], src[:, j, BW * q:BW * (q + 1)], ACT.Square, bias=col(cur, 3),
                                         accum_out=squares[:, K * i + j:K * i + j + 1]).then_inc(pieces_done, 1)
                else:
                    h = j - K
                    v = src[:, 2 * h:2 * h + 2, BW * q:BW * (q + 1)]
                    nc.scalar.activation(v, v, ACT.Identity, bias=col(cur, 3),
                                         accum_out=sums[:, 2 * i + h:2 * i + h + 1]).then_inc(pieces_done, 1)

            def spill(g, i):
                c, b, q = LOWER[i]
                act.wait_ge(pieces_done, NPIECE * g + piece_end[i])
                act.dma_start(ov[chan(g, c), b][:, :, BW * q:BW * (q + 1)], transit[b][:, :, BW * q:BW * (q + 1)]
                              ).then_inc(x1_spilled[(b, q)], 16)

            def store_kept(g, blk):
                c, b, q = blk
                i = KEPT.index(blk)
                act.wait_ge(kept_done, NR * g + 2 * i + 2)
                act.dma_start(ov[chan(g, c), b][:, :, BW * q:BW * (q + 1)], kept[(c, b)][:, :, BW * q:BW * (q + 1)]
                              ).then_inc(kept_stored[blk], 16)

            def scale_stream(g, u):
                c, b, q = STREAM[u // 2]
                v = ubuf[:, u % NUB, :, :]
                act.wait_ge(u_loaded[u % NUB], 16 * (g * (NU // NUB) + u // NUB + 1))
                nc.scalar.activation(v, v, ACT.Identity, bias=0.0 if q <= b else col(outp, 2), scale=col(outp, 0)
                                     ).then_inc(u_scaled, 1)

            def store_stream(g, u):
                (c, b, q), h = STREAM[u // 2], u % 2
                act.wait_ge(u_added, NU * g + u + 1)
                act.dma_start(ov[chan(g, c), b][:, 2 * h:2 * h + 2, BW * q:BW * (q + 1)], ubuf[:, u % NUB, :, :]
                              ).then_inc(u_stored[u % NUB], 16)

            def stage(s, do_a, do_b, do_c):
                gb, gc = s - 1, s - 2
                if do_b:
                    act.wait_ge(gn1_ready, 2 * gb + 2)
                    for n in range(3):
                        norm(gb, n)
                    split_hi(gb, 0)
                    split_hi(gb, 1)
                if do_c:
                    for at, i, j in pieces:
                        if at >= NT:
                            piece(gc, i, j)
                for n in range(NT):
                    if do_b:
                        if n + 3 < NT:
                            norm(gb, n + 3)
                        if n + 2 < NT:
                            split_hi(gb, n + 2)
                        for e, w in EDGES:
                            if e == n:
                                copy_edge(gb, e, w)
                        for at, i, j in pieces:
                            if at == n:
                                piece(gb, i, j)
                        for i, at in spill_pos.items():
                            if at == n:
                                spill(gb, i)
                    if do_a and n == STATS1[3]:
                        act.wait_ge(s1_root, s * 2 + 1)
                        nc.scalar.activation(t1[:, 6:7], t1[:, 5:6], ACT.Sqrt).then_inc(s1_root, 1)
                    if do_c:
                        if n == 3:
                            act.wait_ge(s2_root, gc * 2 + 1)
                            nc.scalar.activation(t2[:, 6:7], t2[:, 5:6], ACT.Sqrt).then_inc(s2_root, 1)
                            act.wait_ge(gn2_ready, gc + 1)
                        for c in range(CPG):
                            if n == BIAS_SHIFT[c]:
                                act.wait_ge(bias_loaded, 16 * (chan(gc, c) + 1))
                                nc.scalar.activation(bias[:, :], bias[:, :], ACT.Identity, bias=col(outp, 1)
                                                     ).then_inc(bias_shifted, 1)
                        for u in range(NU):
                            if u_pos[u] == n:
                                scale_stream(gc, u)
                        for blk in KEPT:
                            if kept_pos[blk][1] + 1 == n:
                                store_kept(gc, blk)
                        for u in range(NU):
                            if min(u_pos[u] + 2, NT - 1) == n:
                                store_stream(gc, u)

            stages(act, stage)
            for blk in KEPT:
                act.wait_ge(kept_stored[blk], 16 * G)
            for i in range(NUB):
                act.wait_ge(u_stored[i], 16 * G * (NU // NUB))
            for s in x1_spilled.values():
                act.wait_ge(s, 16 * CH)

        @block.vector
        def _(dve):
            nc.vector.memset(zeros, 0.0).then_inc(zeros_ready, 1)
            dve.wait_ge(wall_loaded, 16)
            wv = wall.rearrange("p (c i) -> p c i", c=CH)
            hiw, low = squares[:, 0:CH], squares[:, CH:2 * CH]
            nc.vector.tensor_reduce(out=hiw, in_=wv, axis=AX.X, op=ALU.max).then_inc(scale_chain, 1)
            nc.vector.tensor_reduce(out=low, in_=wv, axis=AX.X, op=ALU.min).then_inc(scale_chain, 1)
            dve.wait_ge(scale_chain, 2)
            nc.vector.scalar_tensor_tensor(out=hiw, in0=low, scalar=-1.0, in1=hiw, op0=ALU.mult,
                                           op1=ALU.max).then_inc(scale_chain, 1)
            dve.wait_ge(scale_chain, 3)
            nc.vector.tensor_scalar(low, hiw, 1e-30, None, ALU.max).then_inc(scale_chain, 1)
            dve.wait_ge(scale_chain, 4)
            nc.vector.tensor_scalar(wsc[:, :, 1], low, 1.0 / WSCALE, None, ALU.mult).then_inc(scale_chain, 1)
            dve.wait_ge(scale_chain, 5)
            nc.vector.reciprocal(wsc[:, :, 0], wsc[:, :, 1]).then_inc(scale_chain, 1)
            dve.wait_ge(scale_chain, 6)
            nc.vector.memset(t1[:, 15:16], 0.0).then_inc(scale_chain, 1)

            def split_lo(g, n):
                N = NT * g + n
                dve.wait_ge(hi_ready, N + 1)
                nc.vector.tensor_tensor(XT[:, n % NB3, 1, :, 2:P + 2], psT[n % NB3][:, :, :],
                                        XT[:, n % NB3, 0, :, 2:P + 2], ALU.subtract).then_inc(lo_ready, 1)

            def evict(g, n):
                c, b, t = TILES[n]
                N = NT * g + n
                c0, c1 = (0 if t == 0 else PADC), min(TOUT, BW * (b + 1) - STEP * t)
                y = psY[n % NB3][:, :, c0:c1]
                xs = slot(c, b)[:, :, STEP * t + c0:STEP * t + c1]
                dve.wait_ge(convolved, N + 1)
                if n % NTC == 0:
                    dve.wait_ge(wback_ready, chan(g, c) + 1)
                if is_diag[n]:
                    nc.vector.tensor_tensor(y, y, mask_at(b, t, c0, c1), ALU.mult).then_inc(conv_masked, 1)
                    dve.wait_ge(conv_masked, ND * g + DIAG_BEFORE[n] + 1)
                nc.vector.scalar_tensor_tensor(out=xs, in0=y, scalar=col(wback, c), in1=xs,
                                               op0=ALU.mult, op1=ALU.add).then_inc(evicted, 1)

            def take_stats(g, a):
                c, b, q, h = a_half(a)
                dve.wait_ge(a_loaded[a % NAB], 16 * (g * (NA // NAB) + a // NAB + 1))
                for k in range(2):
                    if q <= b:
                        e = ((c * (NBAND * (NBAND + 1) // 2) + b * (b + 1) // 2 + q) * K) + 2 * h + k
                    else:
                        up = sum(NBAND - 1 - bb for bb in range(b)) + q - b - 1
                        e = LO_ENTRIES + (c * UPPER_PER_CH + up) * K + 2 * h + k
                    last = nc.vector.bn_stats(entries[:, e, :], abuf[:, a % NAB, k, :])
                last.then_inc(a_done, 1)

            def inv_root(v, t, chain, base, root, g):
                dve.wait_ge(root, 2 * g + 2)
                nc.vector.reciprocal(t[:, 7:8], t[:, 6:7]).then_inc(chain, 1)
                dve.wait_ge(chain, base + 1)
                nc.vector.scalar_tensor_tensor(out=t[:, 8:9], in0=t[:, 7:8], scalar=t[:, 5:6], in1=t[:, 6:7],
                                               op0=ALU.mult, op1=ALU.add).then_inc(chain, 1)
                dve.wait_ge(chain, base + 2)
                nc.vector.tensor_scalar(t[:, 8:9], t[:, 8:9], 0.5, None, ALU.mult).then_inc(chain, 1)
                dve.wait_ge(chain, base + 3)
                nc.vector.reciprocal(t[:, 9:10], t[:, 8:9]).then_inc(chain, 1)
                dve.wait_ge(chain, base + 4)

            L1 = 11

            def stats1(g, part):
                base = g * L1
                if part == 0:
                    dve.wait_ge(a_done, NA * (g + 1))
                    nc.vector.memset(t1[:, 14:15], 0.0).then_inc(s1_chain, 1)
                    flat_e = entries[:, :, :].rearrange("p e s -> p (e s)")
                    nc.vector.bn_aggr(t1[:, 0:2], flat_e).then_inc(s1_chain, 1)
                    nc.vector.bn_aggr(nxt[:, 1:3], flat_e[:, LO_ENTRIES * 6:]).then_inc(s1_chain, 1)
                elif part == 1:
                    dve.wait_ge(s1_pool, 2 * g + 1)
                    nc.vector.tensor_scalar(col(nxt, 0), t1[:, 2:3], 1.0 / P, None, ALU.mult).then_inc(s1_chain, 1)
                    dve.wait_ge(s1_chain, base + 4)
                    nc.vector.tensor_tensor(t1[:, 10:11], t1[:, 0:1], col(nxt, 0), ALU.subtract
                                            ).then_inc(s1_chain, 1)
                    dve.wait_ge(s1_chain, base + 5)
                    nc.vector.scalar_tensor_tensor(out=t1[:, 3:4], in0=t1[:, 10:11], scalar=t1[:, 10:11],
                                                   in1=t1[:, 1:2], op0=ALU.mult, op1=ALU.add).then_inc(s1_chain, 1)
                elif part == 2:
                    dve.wait_ge(s1_pool, 2 * g + 2)
                    nc.vector.tensor_scalar(t1[:, 5:6], t1[:, 4:5], 1.0 / P, EPS, ALU.mult, ALU.add
                                            ).then_inc(s1_root, 1)
                else:
                    inv_root(g, t1, s1_chain, base + 6, s1_root, g)
                    nc.vector.scalar_tensor_tensor(out=t1[:, 11:12], in0=t1[:, 9:10], scalar=-1.0, in1=col(nxt, 0),
                                                   op0=ALU.mult, op1=ALU.mult).then_inc(s1_chain, 1)
                    dve.wait_ge(s1_chain, base + 11)

            def hand_over_norm(ga, gb):
                if gb is not None:
                    dve.wait_ge(diag_normed, ND * (gb + 1))
                nc.vector.tensor_copy(normp[:, 0:1], t1[:, 9:10]).then_inc(gn1_ready, 1)
                nc.vector.tensor_copy(normp[:, 1:2], t1[:, 11:12]).then_inc(gn1_ready, 1)

            def hand_over_sums(g):
                nc.vector.tensor_copy(cur[:, 0:3], nxt[:, :]).then_inc(cur_ready, 1)
                nc.vector.tensor_scalar(col(cur, 3), col(nxt, 0), -1.0, None, ALU.mult).then_inc(cur_ready, 1)

            NUP = float(CPG * UPPER_PER_CH * K * BW)
            L2 = 16

            def stats2(g):
                base = g * L2

                def link(i, ins):
                    ins.then_inc(s2_chain, 1)
                    dve.wait_ge(s2_chain, base + i)
                dve.wait_ge(pieces_done, NPIECE * (g + 1))
                wait(dve, u_scaled, NU * g)
                link(1, nc.vector.tensor_reduce(out=t2[:, 0:1], in_=sums[:, :], axis=AX.X, op=ALU.add))
                nc.vector.tensor_reduce(out=t2[:, 1:2], in_=squares[:, :], axis=AX.X, op=ALU.add
                                        ).then_inc(sums_read, 1)
                link(2, nc.vector.tensor_tensor(t2[:, 10:11], col(cur, 1), col(cur, 0), ALU.subtract))
                link(3, nc.vector.scalar_tensor_tensor(out=t2[:, 11:12], in0=t2[:, 10:11], scalar=t2[:, 10:11],
                                                       in1=col(cur, 2), op0=ALU.mult, op1=ALU.add))
                dve.wait_ge(sums_read, g + 1)
                link(4, nc.vector.scalar_tensor_tensor(out=t2[:, 0:1], in0=t2[:, 10:11], scalar=NUP, in1=t2[:, 0:1],
                                                       op0=ALU.mult, op1=ALU.add))
                link(5, nc.vector.scalar_tensor_tensor(out=t2[:, 1:2], in0=t2[:, 11:12], scalar=NUP, in1=t2[:, 1:2],
                                                       op0=ALU.mult, op1=ALU.add))
                dve.wait_ge(s2_pool, g + 1)
                link(6, nc.vector.tensor_scalar(t2[:, 4:5], t2[:, 2:3], 1.0 / ROWN, None, ALU.mult))
                link(7, nc.vector.tensor_tensor(t2[:, 12:13], t2[:, 4:5], t2[:, 4:5], ALU.mult))
                link(8, nc.vector.scalar_tensor_tensor(out=t2[:, 13:14], in0=t2[:, 3:4], scalar=1.0 / ROWN,
                                                       in1=t2[:, 12:13], op0=ALU.mult, op1=ALU.subtract))
                nc.vector.tensor_scalar(t2[:, 5:6], t2[:, 13:14], 0.0, EPS, ALU.max, ALU.add).then_inc(s2_root, 1)
                inv_root(g, t2, s2_chain, base + 8, s2_root, g)
                link(13, nc.vector.tensor_scalar(col(outp, 0), t2[:, 9:10], 1.0, None, ALU.add))
                link(14, nc.vector.tensor_tensor(t2[:, 14:15], t2[:, 9:10], t2[:, 4:5], ALU.mult))
                link(15, nc.vector.tensor_tensor(col(outp, 1), col(cur, 0), t2[:, 14:15], ALU.subtract))
                link(16, nc.vector.tensor_tensor(col(outp, 2), col(outp, 0), col(cur, 3), ALU.mult))
                nc.vector.tensor_copy(t2[:, 15:16], t2[:, 9:10]).then_inc(gn2_ready, 1)

            def build_weights(g, c):
                sc = wsc[:, bass.ds(chan(g, c), 1), 0]
                dve.wait_ge(w_loaded, 16 * K * (chan(g, c) + 1))
                wait(dve, convolved, NT * g if c else NT * (g - 1) + NTC)
                if isinstance(g, int) and g == 0 and c == 0:
                    dve.wait_ge(scale_chain, 7)
                nc.vector.tensor_copy(col(wback, c), wsc[:, bass.ds(chan(g, c), 1), 1]).then_inc(wback_ready, 1)
                nc.vector.tensor_scalar(wsplit[:, c, 0, :, :], wstage[:, :, :], sc, None, ALU.mult
                                        ).then_inc(w_hi_built, 1)
                dve.wait_ge(w_hi_built, chan(g, c) + 1)
                nc.vector.scalar_tensor_tensor(out=wsplit[:, c, 1, :, :], in0=wstage[:, :, :], scalar=sc,
                                               in1=wsplit[:, c, 0, :, :], op0=ALU.mult, op1=ALU.subtract
                                               ).then_inc(w_built, 1)

            def finish_kept(g, blk, h):
                c, b, q = blk
                if h == 0:
                    dve.wait_ge(bias_shifted, chan(g, c) + 1)
                v = kept[(c, b)][:, 2 * h:2 * h + 2, BW * q:BW * (q + 1)]
                nc.vector.scalar_tensor_tensor(out=v, in0=v, scalar=col(outp, 0), in1=bias_at(b, q, h),
                                               op0=ALU.mult, op1=ALU.add).then_inc(kept_done, 1)

            def stage(s, do_a, do_b, do_c):
                ga, gb, gc = s, s - 1, s - 2
                if do_b:
                    split_lo(gb, 0)
                    split_lo(gb, 1)
                for n in range(NT):
                    if do_b:
                        if n + 2 < NT:
                            split_lo(gb, n + 2)
                        if n >= 1:
                            evict(gb, n - 1)
                    if do_c:
                        if n == 3:
                            stats2(gc)
                        for blk in KEPT:
                            for h in range(2):
                                if kept_pos[blk][h] == n:
                                    finish_kept(gc, blk, h)
                    if do_a:
                        for a in range(NA):
                            if a_pos[a] == n:
                                take_stats(ga, a)
                        if n in STATS1:
                            stats1(ga, STATS1.index(n))
                        if n == W_BUILD[0]:
                            build_weights(ga, 0)
                        if n == HAND_OVER_NORM:
                            hand_over_norm(ga, gb if do_b else None)
                    if do_b and n == HAND_OVER_SUMS:
                        hand_over_sums(gb)
                    if do_b and n == W_BUILD[1]:
                        build_weights(gb, 1)
                if do_b:
                    evict(gb, NT - 1)

            stages(dve, stage)

        @block.gpsimd
        def _(pool):
            nc.gpsimd.iota(pos_in, pattern=[[1, NPOS]], base=-(HH - 1), channel_multiplier=0,
                           allow_small_or_imprecise_dtypes=True).then_inc(pos_ready, 1)
            nc.gpsimd.memset(mask[:, :], 1.0).then_inc(const_ready, 1)
            nc.gpsimd.memset(ident[:, :], 0.0).then_inc(const_ready, 1)
            nc.gpsimd.memset(xn[:, :, :, :, :], 0.0).then_inc(const_ready, 1)
            nc.gpsimd.memset(wstage[:, :, :], 0.0).then_inc(const_ready, 1)
            pool.wait_ge(const_ready, 4)
            nc.gpsimd.affine_select(out=mask[:, :], in_=mask[:, :], pattern=[[1, MW]], compare_op=ALU.is_ge,
                                    fill=0.0, base=MLO, channel_multiplier=K).then_inc(const_ready, 1)
            nc.gpsimd.affine_select(out=ident[:, :], in_=ident[:, :], pattern=[[-1, P]], compare_op=ALU.not_equal,
                                    fill=1.0, base=0, channel_multiplier=1).then_inc(const_ready, 1)
            pool.wait_ge(const_ready, 6)

            def mask_tile(g, n):
                c, b, t = TILES[n]
                pool.wait_ge(diag_normed, ND * g + DIAG_BEFORE[n] + 1)
                v = xn[:, n % NB3, :, :, :]
                m = mask_at(b, t, 0, TIN)
                m = bass.AP(m.tensor, m.offset, [m.ap[0], [-XC, NPC], [1, K], [-1, XC]])
                nc.gpsimd.tensor_tensor(v, v, m, ALU.mult).then_inc(xn_ready, 1)

            def halos(g, n):
                c, b, t = TILES[n]
                N = NT * g + n
                if n % NTC == 0:
                    wait_alone(pool, halo_out, N)
                    nc.gpsimd.memset(halo[:, :, :, :, :], 0.0).then_inc(halo_zeroed, 1)
                    wait_alone(pool, halo_zeroed, chan(g, c) + 1)
                wait_alone(pool, convolved, N - NB3 + 1)
                wait_alone(pool, halo_out, N - NB3 + 1)
                for e, _ in EDGES:
                    if n > e and (c, t) == (TILES[e][0], TILES[e][2] + 1):
                        wait_alone(pool, edge_copied, 16 * K * (NEDGE * g + edges_before(n)))
                nc.gpsimd.tensor_copy(XT[:, n % NB3, :, :, 0:2], halo[:, t, :, :, :]).then_inc(halo_in, 1)
                wait_alone(pool, halo_in, N + 1)
                wait_alone(pool, lo_ready, N + 1)
                nc.gpsimd.tensor_copy(halo[:, t, :, :, :], XT[:, n % NB3, :, :, P:P + 2]).then_inc(halo_out, 1)

            def add_bias(g, u):
                (c, b, q), h = STREAM[u // 2], u % 2
                pool.wait_ge(bias_shifted, chan(g, c) + 1)
                pool.wait_ge(u_scaled, NU * g + u + 1)
                v = ubuf[:, u % NUB, :, :]
                nc.gpsimd.tensor_tensor(v, v, bias_at(b, q, h), ALU.add).then_inc(u_added, 1)

            def stage(s, do_a, do_b, do_c):
                ga, gb, gc = s, s - 1, s - 2
                if do_b:
                    for n in range(3):
                        if is_diag[n]:
                            mask_tile(gb, n)
                    halos(gb, 0)
                    halos(gb, 1)
                for n in range(NT):
                    if do_b:
                        if n + 3 < NT and is_diag[n + 3]:
                            mask_tile(gb, n + 3)
                        if n + 2 < NT:
                            halos(gb, n + 2)
                    if do_a and n == STATS1[0]:
                        wait_alone(pool, s1_chain, 11 * ga + 3)
                        nc.gpsimd.partition_all_reduce(t1[:, 2:3], t1[:, 0:1], P, RED.add).then_inc(s1_pool, 1)
                    if do_a and n == STATS1[1]:
                        wait_alone(pool, s1_chain, 11 * ga + 6)
                        nc.gpsimd.partition_all_reduce(t1[:, 4:5], t1[:, 3:4], P, RED.add).then_inc(s1_pool, 1)
                    if do_c:
                        if n == 3:
                            wait_alone(pool, s2_chain, 16 * gc + 5)
                            nc.gpsimd.partition_all_reduce(t2[:, 2:4], t2[:, 0:2], P, RED.add).then_inc(s2_pool, 1)
                        for u in range(NU):
                            if u_pos[u] == n:
                                add_bias(gc, u)

            stages(pool, stage)

        @block.tensor
        def _(pe):
            pe.wait_ge(small_loaded, 96)
            pe.wait_ge(h1_ready, 1)
            for j in range(NPOS // BW):
                cols = slice(j * BW, (j + 1) * BW)
                if j >= 2:
                    pe.wait_ge(h2_ready, j - 1)
                nc.tensor.matmul(psT[j % 2][0:DIM, :, :].rearrange("p a b -> p (a b)"), w2s[:, :], h1[:, cols],
                                 start=True, stop=True).then_inc(mlp2_done, 1)
                pe.wait_ge(h2_ready, j + 1)
                if j >= 2:
                    pe.wait_ge(table_ready, j - 1)
                nc.tensor.matmul(psY[j % 2][0:CH, :, :].rearrange("p a b -> p (a b)"), w3s[:, :], h2[:, cols],
                                 start=True, stop=True).then_inc(mlp3_done, 1)
            pe.wait_ge(table_ready, 8)
            pe.wait_ge(const_ready, 6)

            def transpose(N, m):
                wait(pe, lo_ready, N - NB3 + 1)
                pe.wait_ge(xn_ready, N + 1)
                for i in range(NPC):
                    last = nc.tensor.transpose(psT[m][:, i, :], xn[:, m, i, :, :].rearrange("p k c -> p (k c)"), ident[:, :])
                last.then_inc(transposed, 1)

            def convolve(N, m, c):
                pe.wait_ge(lo_ready, N + 1)
                pe.wait_ge(halo_in, N + 1)
                wait(pe, evicted, N - NB3 + 1)
                products = [(i, sh, xp, wp) for i in range(NPC) for sh in range(3)
                            for xp, wp in ((0, 0), (0, 1), (1, 0))]
                for j, (i, sh, xp, wp) in enumerate(products):
                    lo_c = max(0, PADC - XC * i)
                    hi_c = min(WC, TOUT + PADC - XC * i)
                    rows = min(K, NE - K * sh)
                    o = XC * i - PADC
                    last = nc.tensor.matmul(psY[m][:, 0:rows, o + lo_c:o + hi_c],
                                            XT[:, m, xp, i, 2 - sh:2 - sh + P],
                                            wsplit[:, c, wp, K * sh:K * sh + rows, lo_c:hi_c],
                                            start=(j == 0), stop=(j == len(products) - 1), skip_group_check=True)
                last.then_inc(convolved, 1)

            def triple(N, c, ahead):
                for i in range(NB3):
                    convolve(N + i, i, c)
                    if i < ahead:
                        transpose(N + i + 2, (i + 2) % NB3)

            def group(g):
                first = NT * g
                transpose(first, 0)
                transpose(first + 1, 1)
                pe.wait_ge(w_built, chan(g, 0) + 1)
                triple(first, 0, 3)
                with pe.Fori(1, NTC // NB3) as j:
                    triple(first + NB3 * j, 0, 3)
                pe.wait_ge(w_built, chan(g, 1) + 1)
                triple(first + NTC, 1, 3)
                with pe.Fori(NTC // NB3 + 1, 2 * NTC // NB3 - 1) as j:
                    triple(first + NB3 * j, 1, 3)
                triple(first + NT - NB3, 1, 1)

            group(0)
            with pe.Fori(1, G) as g:
                group(g)


_INS = ["x", "w", "w1", "b1", "w2", "b2", "w3", "b3"]


def kernel(x, L0_conv_weight, L1_conv_W1, L1_conv_b1, L1_conv_W2, L1_conv_b2, L1_conv_W3, L1_conv_b3):
    import numpy as _np
    import concourse.bacc as _bacc
    from concourse import mybir as _mybir
    from concourse.bass_utils import run_bass_kernel_spmd as _run

    nc = _bacc.Bacc("TRN2", target_bir_lowering=False, num_devices=1)
    values = [x, _np.asarray(L0_conv_weight)[:, ::-1, ::-1], L1_conv_W1, L1_conv_b1, L1_conv_W2, L1_conv_b2,
              L1_conv_W3, L1_conv_b3]
    arrays, args = {}, []
    for name, v in zip(_INS, values):
        a = _np.ascontiguousarray(v)
        arrays[f"in_{name}"] = a
        args.append(nc.dram_tensor(f"in_{name}", a.shape, _mybir.dt.from_np(a.dtype), kind="ExternalInput").ap())
    out = nc.dram_tensor("out_0", x.shape, _mybir.dt.float32, kind="ExternalOutput").ap()
    preact_conv_kernel(nc, *args, out)
    r = _run(nc, [arrays], core_ids=[0])
    return r.results[0]["out_0"]
```

```python
import concourse.bass as bass
from concourse import mybir
from contextlib import ExitStack


def preact_conv_kernel(nc, x, wflip, w1, b1, w2, b2, w3, b3, out):
    f32, f16, bf16 = mybir.dt.float32, mybir.dt.float16, mybir.dt.bfloat16
    ALU = mybir.AluOpType
    ACT = mybir.ActivationFunctionType
    AX = mybir.AxisListType
    RED = bass.bass_isa.ReduceOp

    _, CH, HH, WW = x.shape
    _, TR, TS = wflip.shape
    DIM = w2.shape[0]
    P, K, BW = 128, 4, 512
    CPG = 2
    G = CH // CPG
    NBAND = HH // (P * K)
    XC = P // K
    NPC = 4
    TIN = NPC * XC
    PADC = TS // 2
    TOUT = TIN - PADC
    STEP = TIN - 2 * PADC
    WC = XC + TS - 1
    NE = TR + K - 1
    ROWN = P * CPG * HH * WW // P
    NPP = ROWN // P
    EPS = 1e-5
    WSCALE = 256.0
    NB3 = 3
    AHEAD = 4

    def band_tiles(b):
        return -(-(BW * (b + 1) - TOUT) // STEP) + 1
    TILES = [(c, b, t) for c in range(CPG) for b in range(NBAND) for t in range(band_tiles(b))]
    NT = len(TILES)
    NTC = NT // CPG
    MAXT = band_tiles(NBAND - 1)
    is_diag = [STEP * t + TIN > BW * b for c, b, t in TILES]
    DIAG_BEFORE = [sum(is_diag[:n]) for n in range(NT + 1)]
    ND = DIAG_BEFORE[NT]

    EDGES = [(n, BW * (b + 1) - STEP * (t + 1)) for n, (c, b, t) in enumerate(TILES)
             if b < NBAND - 1 and t == band_tiles(b) - 1 and BW * (b + 1) > STEP * (t + 1)]
    assert all(w <= XC - STEP % XC for _, w in EDGES)
    edges_before = lambda n: sum(e < n for e, _ in EDGES)
    NEDGE = len(EDGES)

    LOWER = [(c, b, q) for c in range(CPG) for b in range(NBAND) for q in range(b + 1)]
    NL = len(LOWER)
    first_tile = {blk: next(n for n, (c, b, t) in enumerate(TILES)
                            if (c, b) == blk[:2] and STEP * t + TIN > BW * blk[2]) for blk in LOWER}
    last_tile = {blk: next(n for n, (c, b, t) in enumerate(TILES)
                           if (c, b) == blk[:2] and STEP * t + TOUT >= BW * (blk[2] + 1)) for blk in LOWER}
    KEPT = [blk for blk in LOWER if blk[1] >= 2]
    STREAM = [(c, b, q) for c in range(CPG) for b in range(NBAND) for q in range(NBAND)
              if (c, b, q) not in KEPT]
    NU = 2 * len(STREAM)
    NR = 2 * len(KEPT)
    A_HALVES = [(c, b, q, h) for c in range(CPG) for b in range(NBAND) for q in range(NBAND) for h in range(2)]
    A_EARLY = [x for x in A_HALVES if x[0] == 0 and x[1] < 2 and x[2] <= x[1]]
    A_STREAM = [x for x in A_HALVES if x not in A_EARLY]
    NA = len(A_STREAM)
    NAB, NUB = 4, 4
    UPPER_PER_CH = NBAND * (NBAND - 1) // 2
    LO_ENTRIES = CPG * (NBAND * NBAND - UPPER_PER_CH) * K

    BIAS_LOAD, BIAS_SHIFT = {1: 44}, {0: 2, 1: 47}
    NEXT_BIAS_LOAD = 88
    TRANSIT_LOAD = {1: {(0, 0): 24, (1, 0): 31, (1, 1): 37}, 0: {(0, 0): 60, (1, 0): 66, (1, 1): 69}}
    EARLY_STATS = 71
    W_LOAD, W_BUILD = {1: 10, 0: 55}, {1: 20, 0: 65}
    STATS1, HAND_OVER_NORM, STATS2, HAND_OVER_SUMS = (79, 80, 81, 82), 85, 2, 5
    parts = [(i, 0, BW, last_tile[blk]) for i, blk in enumerate(LOWER)]
    split = STEP * (MAXT - 3) + TOUT - BW * (NBAND - 1)
    parts[-1:] = [(NL - 1, 0, split, NT - 3), (NL - 1, split, BW, NT - 1)]
    PIECES = []
    at, used = 0, 0
    for i, c0, c1, done in parts:
        wide = 2 * (c1 - c0) > BW
        todo = [(True, r, 1 if wide else 2) for r in range(0, K, 1 if wide else 2)]
        todo += [(False, r, 2 if wide else K) for r in range(0, K, 2 if wide else K)]
        for sq, r, nr in todo:
            if done + 2 > at:
                at, used = done + 2, 0
            elif used == 2 and at < NT - 1:
                at, used = at + 1, 0
            used += 1
            PIECES.append((at, i, sq, r, nr, c0, c1))
    NPIECE = len(PIECES)
    NSQ = sum(x[2] for x in PIECES)
    piece_end = {i: max(j for j, x in enumerate(PIECES) if x[1] == i) + 1 for i in range(NL)}
    spill_pos = {i: PIECES[piece_end[i] - 1][0] + 1 for i in range(NL) if LOWER[i][1] < 2}

    KEPT_LEAD = 13
    kept_pos = {}
    for blk in KEPT:
        at = max(3, first_tile[blk] - KEPT_LEAD)
        kept_pos[blk] = (at, at + 1)
    traffic = [0.0] * (NT + 8)

    def book(at, megabytes, over):
        for i in range(over):
            traffic[at + i] += megabytes / over
    for blk in KEPT:
        book(kept_pos[blk][1] + 1, 1.0, 2)
        book(kept_pos[blk][1] + 4, 1.0, 2)
    for at in spill_pos.values():
        book(at, 1.0, 2)
    for at in (at for of in TRANSIT_LOAD.values() for at in of.values()):
        book(at, 1.0, 2)
    for at in (BIAS_LOAD[1], NEXT_BIAS_LOAD):
        book(at, 1.8, 2)

    def spread(count, lo, hi, level):
        room = [max(0.05, level - traffic[n]) for n in range(lo, hi + 1)]
        out, acc, n = [], room[0], 0
        for i in range(count):
            while acc < (i + 0.5) * sum(room) / count:
                n += 1
                acc += room[n]
            out.append(lo + n)
        return out
    u_pos = spread(NU // 2, 4, 42, 1.6) + spread(NU // 2, 49, 87, 1.6)
    for n in u_pos:
        book(max(0, n - 2), 0.5, 2)
        book(n + 2, 0.5, 2)
    a_pos = spread(NA, 0, 77, 1.3)
    a_load_pos = [0 if a < NAB else a_pos[a - NAB] + 1 for a in range(NA)]
    u_load_pos = [(0 if i < NUB else u_pos[i - NUB] + 3) for i in range(NU)]

    xv = x.rearrange("o c (b p k) w -> (o c) b p k w", p=P, k=K)
    ov = out.rearrange("o c (b p k) w -> (o c) b p k w", p=P, k=K)
    taps_dram = nc.dram_tensor("taps_scratch", [CH * TR, XC * WC], f32, kind="Internal").ap()
    taps_v = taps_dram.rearrange("(c r) (p j) -> c p r j", r=TR, j=WC)
    NPOS = 2 * HH
    bias_dram = nc.dram_tensor("bias_scratch", [CH, NPOS], f32, kind="Internal").ap()
    VLO = -(WW - 1)
    NV = BW * (NBAND - 1) + K - 1 - VLO + 1

    ctx = ExitStack()
    with ctx:
        def sb(name, shape, dt):
            return ctx.enter_context(nc.sbuf_tensor(name, shape, dt))

        def sem(name):
            return ctx.enter_context(nc.semaphore(name))

        transit = {b: sb(f"band{b}", [P, K, BW * (b + 1)], f32) for b in (0, 1)}
        kept = {(c, b): sb(f"kept_c{c}_band{b}", [P, K, BW * (b + 1)], f32)
                for c in range(CPG) for b in (2, 3)}

        def slot(c, b):
            return transit[b] if b < 2 else kept[(c, b)]

        bias = sb("bias", [P, NV], f32)
        abuf = sb("abuf", [P, NAB, 2, BW], f32)
        ubuf = sb("ubuf", [P, NUB, 2, BW], f32)
        xn = sb("xn", [P, NB3, NPC, K, XC], f32)
        XT = sb("XT", [P, NB3, 2, NPC, P + 2], f16)
        halo = sb("halo", [P, MAXT, 2, NPC, 2], f16)
        wstage = sb("wstage", [P, NE, WC], f32)
        wsplit = sb("wsplit", [P, CPG, 2, NE, WC], f16)
        MLO = BW * 0 - STEP * (band_tiles(0) - 1) - (TIN - 1)
        MW = 728
        mask = sb("mask", [P, MW], bf16)
        ident = sb("ident", [P, P], f32)
        entries = sb("entries", [P, 2 * len(A_HALVES), 6], f32)
        nxt = sb("nxt", [P, 3], f32)
        normp = sb("normp", [P, 2], f32)
        cur = sb("cur", [P, 4], f32)
        outp = sb("outp", [P, 2], f32)
        wback = sb("wback", [P, CPG], f32)

        def col(t, i):
            return t[:, i:i + 1]
        wsc = sb("wsc", [P, CH, 2], f32)
        sums = sb("sums", [P, NPIECE - NSQ], f32)
        squares = sb("squares", [P, NSQ], f32)
        t1 = sb("t1", [P, 16], f32)
        t2 = sb("t2", [P, 16], f32)
        small = sb("small", [DIM, 8], f32)
        w2s = sb("w2s", [DIM, DIM], f32)
        w3s = sb("w3s", [DIM, CH], f32)
        psT = [ctx.enter_context(nc.psum_tensor(f"psT{i}", [P, NPC, P], f32)) for i in range(NB3)]
        psY = [ctx.enter_context(nc.psum_tensor(f"psY{i}", [P, K, TIN], f32)) for i in range(NB3)]
        junk = ctx.enter_context(nc.psum_tensor("junk", [P, BW], f32))

        def flat(t):
            return t[:, :, :].rearrange("p a b -> p (a b)")
        pos_in = flat(kept[(0, 3)])[0:DIM, 0:NPOS]
        h1 = flat(kept[(0, 3)])[0:DIM, NPOS:2 * NPOS]
        h2 = flat(kept[(1, 3)])[0:DIM, 0:NPOS]
        table = flat(kept[(1, 3)])[0:CH, NPOS:2 * NPOS]
        zeros = flat(kept[(0, 2)])[0:CH * TR, 0:XC * WC]
        wall = flat(kept[(1, 2)])[:, 0:CH * TR * TS]

        const_ready = sem("const_ready")
        small_loaded = sem("small_loaded")
        wall_loaded = sem("wall_loaded")
        zeros_ready = sem("zeros_ready")
        taps_zeroed = sem("taps_zeroed")
        taps_stored = sem("taps_stored")
        pos_ready = sem("pos_ready")
        h1_ready = sem("h1_ready")
        mlp2_done = sem("mlp2_done")
        h2_ready = sem("h2_ready")
        mlp3_done = sem("mlp3_done")
        table_ready = sem("table_ready")
        table_stored = sem("table_stored")
        scale_chain = sem("scale_chain")
        a_loaded = [sem(f"a_loaded{i}") for i in range(NAB)]
        a_done = sem("a_done")
        early_done = sem("early_done")
        x_loaded = {}
        for c, b, q in LOWER:
            x_loaded[(c, b, q)] = sem(f"x_loaded_{c}{b}{q}") if b >= 2 or c == 0 else x_loaded[(0, b, q)]
        x1_spilled = {(b, q): sem(f"x1_spilled_{b}{q}") for b in (0, 1) for q in range(b + 1)}
        kept_stored = {blk: sem("kept_stored_%d%d%d" % blk) for blk in KEPT}
        u_loaded = [sem(f"u_loaded{i}") for i in range(NUB)]
        u_scaled = sem("u_scaled")
        u_added = sem("u_added")
        u_finished = sem("u_finished")
        u_stored = [sem(f"u_stored{i}") for i in range(NUB)]
        kept_done = sem("kept_done")
        bias_loaded = sem("bias_loaded")
        bias_shifted = sem("bias_shifted")
        w_loaded = sem("w_loaded")
        w_built = sem("w_built")
        w_hi_built = sem("w_hi_built")
        wback_ready = sem("wback_ready")
        diag_normed = sem("diag_normed")
        xn_ready = sem("xn_ready")
        transposed = sem("transposed")
        hi_ready = sem("hi_ready")
        lo_ready = sem("lo_ready")
        halo_zeroed = sem("halo_zeroed")
        halo_in = sem("halo_in")
        halo_out = sem("halo_out")
        edge_copied = sem("edge_copied")
        convolved = sem("convolved")
        conv_masked = sem("conv_masked")
        evicted = sem("evicted")
        pieces_done = sem("pieces_done")
        sums_read = sem("sums_read")
        s1_chain = sem("s1_chain")
        s1_pool = sem("s1_pool")
        s1_root = sem("s1_root")
        s2_chain = sem("s2_chain")
        s2_pool = sem("s2_pool")
        s2_root = sem("s2_root")
        gn1_ready = sem("gn1_ready")
        cur_ready = sem("cur_ready")
        gn2_ready = sem("gn2_ready")

        def chan(g, c):
            return CPG * g + c

        def wait(eng, s, value):
            if not isinstance(value, int) or value > 0:
                eng.wait_ge(s, value)

        def wait_alone(eng, s, value):
            if not isinstance(value, int) or value > 0:
                eng.wait_ge(s, value)
                eng.nop(nofuse=True)

        def bias_at(b, q, h):
            start = 2 * h + BW * b - BW * q - VLO
            full = bias[:, :]
            return bass.AP(full.tensor, start, [[full.ap[0][0], P], [1, 2], [-1, BW]])

        def mask_at(b, t, c0, c1):
            start = BW * b - STEP * t - c0 - MLO
            full = mask[:, :]
            return bass.AP(full.tensor, start, [[full.ap[0][0], P], [1, K], [-1, c1 - c0]])

        block = ctx.enter_context(nc.Block())

        def stages(eng, stage):
            stage(0, True, False, False)
            stage(1, True, True, False)
            with eng.Fori(2, G) as s:
                stage(s, True, True, True)
            stage(G, False, True, True)
            stage(G + 1, False, False, True)

        @block.sync
        def _(sp):
            sp.dma_start(small[:, 0:1], w1.rearrange("o d -> d o")).then_inc(small_loaded, 16)
            sp.dma_start(small[:, 1:2], b1.rearrange("(d o) -> d o", o=1)).then_inc(small_loaded, 16)
            sp.dma_start(small[:, 2:3], b2.rearrange("(d o) -> d o", o=1)).then_inc(small_loaded, 16)
            sp.dma_start(small[0:CH, 3:4], b3.rearrange("(d o) -> d o", o=1)).then_inc(small_loaded, 16)
            sp.dma_start(w2s[:, :], w2).then_inc(small_loaded, 16)
            sp.dma_start(w3s[:, :], w3).then_inc(small_loaded, 16)
            wf = wflip.rearrange("c r s -> (c r s)")
            sp.dma_start(wall, wf.partition_broadcast(P)).then_inc(wall_loaded, 16)
            sp.wait_ge(zeros_ready, 1)
            sp.dma_start(taps_dram[:, :], zeros).then_inc(taps_zeroed, 16)
            sp.wait_ge(taps_zeroed, 16)
            sp.dma_start(bass.AP(taps_dram.tensor, 0, [[XC * WC, CH * TR], [WC + 1, XC], [1, TS]]),
                         bass.AP(wflip.tensor, 0, [[TS, CH * TR], [0, XC], [1, TS]])).then_inc(taps_stored, 16)

            def stage(s, do_a, do_b, do_c):
                ga, gb, gc = s, s - 1, s - 2
                if isinstance(s, int) and s == 1:
                    sp.wait_ge(table_ready, 8)
                    sp.dma_start(bias_dram[:, :], table).then_inc(table_stored, 16)
                    sp.wait_ge(table_stored, 16)
                    sp.wait_ge(scale_chain, 7)
                for n in range(NT):
                    if do_a:
                        for a in range(NA):
                            if a_load_pos[a] == n:
                                c, b, q, h = A_STREAM[a]
                                wait_alone(sp, a_done, ga * NA + (a - NAB + 1 if a >= NAB else 0))
                                sp.dma_start(abuf[:, a % NAB, :, :],
                                             xv[chan(ga, c), b][:, 2 * h:2 * h + 2, BW * q:BW * (q + 1)]
                                             ).then_inc(a_loaded[a % NAB], 16)
                    if do_b:
                        load_transit(gb, 1, n)
                        for blk in KEPT:
                            if kept_pos[blk][1] + 4 == n:
                                c, b, q = blk
                                wait_alone(sp, kept_stored[blk], 16 * gb)
                                sp.dma_start(kept[(c, b)][:, :, BW * q:BW * (q + 1)],
                                             xv[chan(gb, c), b][:, :, BW * q:BW * (q + 1)]
                                             ).then_inc(x_loaded[blk], 16)
                        if n == W_LOAD[1]:
                            load_taps(gb, 1)
                    if do_a and n == W_LOAD[0]:
                        load_taps(ga, 0)
                    if do_a:
                        load_transit(ga, 0, n)
                    if do_c:
                        for u in range(NU):
                            if u_load_pos[u] == n:
                                (c, b, q), h = STREAM[u // 2], u % 2
                                wait_alone(sp, u_stored[u % NUB], 16 * (gc * (NU // NUB) + u // NUB))
                                spilled = q <= b
                                if spilled:
                                    wait_alone(sp, x1_spilled[(b, q)], 16 * (chan(gc, c) + 1))
                                src = (ov if spilled else xv)[chan(gc, c), b]
                                sp.dma_start(ubuf[:, u % NUB, :, :], src[:, 2 * h:2 * h + 2, BW * q:BW * (q + 1)]
                                             ).then_inc(u_loaded[u % NUB], 16)
                        if n == BIAS_LOAD[1]:
                            load_bias(gc, 1)
                    if do_b and n == NEXT_BIAS_LOAD:
                        load_bias(gb, 0)

            def load_transit(g, c, n):
                for (b, q), at in TRANSIT_LOAD[c].items():
                    if at == n:
                        wait_alone(sp, x1_spilled[(b, q)], 16 * chan(g, c))
                        sp.dma_start(transit[b][:, :, BW * q:BW * (q + 1)],
                                     xv[chan(g, c), b][:, :, BW * q:BW * (q + 1)]
                                     ).then_inc(x_loaded[(c, b, q)], 16)

            def load_taps(g, c):
                sp.wait_ge(taps_stored, 16)
                wait_alone(sp, w_built, chan(g, c))
                if isinstance(g, int) and g == 0 and c == 0:
                    sp.wait_ge(const_ready, 6)
                for k in range(K):
                    sp.dma_start(wstage[XC * k:XC * (k + 1), k:k + TR, :], taps_v[chan(g, c)]
                                 ).then_inc(w_loaded, 16)

            def load_bias(g, c):
                wait_alone(sp, kept_done, g * NR + c * (NR // 2))
                for done in (u_added, u_finished):
                    wait_alone(sp, done, (g * NU + c * (NU // 2)) // 2)
                row = bias_dram[bass.ds(chan(g, c), 1), :]
                src = bass.AP(row.tensor, row.offset, [[K, P], [1, NV]])
                sp.dma_start(bias[:, :], src).then_inc(bias_loaded, 16)

            stages(sp, stage)

        @block.scalar
        def _(act):
            act.wait_ge(small_loaded, 96)
            act.wait_ge(pos_ready, 1)
            act.wait_ge(const_ready, 6)
            nc.scalar.activation(h1, pos_in, ACT.Relu, bias=small[:, 1:2], scale=small[:, 0:1]).then_inc(h1_ready, 1)
            for j in range(NPOS // BW):
                cols = slice(j * BW, (j + 1) * BW)
                act.wait_ge(mlp2_done, j + 1)
                nc.scalar.activation(h2[:, cols], psT[j % 2][0:DIM, :, :].rearrange("p a b -> p (a b)"),
                                     ACT.Relu, bias=small[:, 2:3]).then_inc(h2_ready, 1)
                act.wait_ge(mlp3_done, j + 1)
                nc.scalar.activation(table[:, cols], psY[j % 2][0:CH, :, :].rearrange("p a b -> p (a b)"),
                                     ACT.Identity, bias=small[0:CH, 3:4]).then_inc(table_ready, 1)

            def norm(g, n):
                c, b, t = TILES[n]
                N = NT * g + n
                for q in range(b + 1):
                    if first_tile[(c, b, q)] == n:
                        act.wait_ge(x_loaded[(c, b, q)], 16 * (g + 1) if b >= 2 else 16 * (chan(g, c) + 1))
                wait(act, transposed, N - NB3 + 1)
                if n > 0 and is_diag[n - 1] and not is_diag[n]:
                    act.wait_ge(xn_ready, N)
                width = min(TIN, BW * (b + 1) - STEP * t)
                whole, rest = divmod(width, XC)
                to = xn[:, n % NB3, :, :, :].rearrange("p i k c -> p k i c")
                x0 = STEP * t
                last = nc.scalar.activation(to[:, :, 0:whole, :], slot(c, b)[:, :, x0:x0 + XC * whole].rearrange(
                    "p k (i c) -> p k i c", c=XC), ACT.Identity, bias=col(normp, 1), scale=col(normp, 0))
                if rest:
                    last = nc.scalar.activation(to[:, :, whole, 0:rest], slot(c, b)[:, :, x0 + XC * whole:x0 + width],
                                                ACT.Identity, bias=col(normp, 1), scale=col(normp, 0))
                last.then_inc(diag_normed if is_diag[n] else xn_ready, 1)

            def split_hi(g, n):
                N = NT * g + n
                act.wait_ge(transposed, N + 1)
                wait(act, convolved, N - NB3 + 1)
                wait(act, halo_out, N - NB3 + 1)
                for e, _ in EDGES:
                    if n == e + NB3:
                        act.wait_ge(edge_copied, 16 * K * (NEDGE * g + edges_before(n)))
                nc.scalar.copy(XT[:, n % NB3, 0, :, 2:P + 2], psT[n % NB3][:, :, :]).then_inc(hi_ready, 1)

            def copy_edge(g, n, w):
                c, b, t = TILES[n]
                act.wait_ge(lo_ready, NT * g + n + 1)
                act.wait_ge(halo_zeroed, chan(g, c) + 1)
                piece_i, col = divmod(STEP, XC)
                for k in range(K):
                    act.dma_start(halo[XC * k:XC * k + w, t + 1, :, 0, :],
                                  XT[XC * k + col:XC * k + col + w, n % NB3, :, piece_i, P:P + 2]
                                  ).then_inc(edge_copied, 16)

            def piece(g, j):
                _, i, sq, r, nr, c0, c1 = PIECES[j]
                c, b, q = LOWER[i]
                done = next(d for ii, a0, _, d in parts if (ii, a0) == (i, c0))
                act.wait_ge(evicted, NT * g + done + 1)
                if j == 0:
                    act.wait_ge(cur_ready, 2 * g + 2)
                    wait(act, sums_read, g)
                wait(act, pieces_done, NPIECE * g + j)
                v = slot(c, b)[:, r:r + nr, BW * q + c0:BW * q + c1]
                k = sum(x[2] == sq for x in PIECES[:j])
                if sq:
                    nc.scalar.activation(junk[:, 0:nr * (c1 - c0)].rearrange("p (r c) -> p r c", r=nr), v, ACT.Square,
                                         bias=col(cur, 3), accum_out=squares[:, k:k + 1]).then_inc(pieces_done, 1)
                else:
                    nc.scalar.activation(v, v, ACT.Identity,
                                         accum_out=sums[:, k:k + 1]).then_inc(pieces_done, 1)

            def spill(g, i):
                c, b, q = LOWER[i]
                act.wait_ge(pieces_done, NPIECE * g + piece_end[i])
                act.dma_start(ov[chan(g, c), b][:, :, BW * q:BW * (q + 1)], transit[b][:, :, BW * q:BW * (q + 1)]
                              ).then_inc(x1_spilled[(b, q)], 16)

            def store_kept(g, blk):
                c, b, q = blk
                i = KEPT.index(blk)
                act.wait_ge(kept_done, NR * g + 2 * i + 2)
                act.dma_start(ov[chan(g, c), b][:, :, BW * q:BW * (q + 1)], kept[(c, b)][:, :, BW * q:BW * (q + 1)]
                              ).then_inc(kept_stored[blk], 16)

            def scale_stream(g, u):
                c, b, q = STREAM[u // 2]
                v = ubuf[:, u % NUB, :, :]
                act.wait_ge(u_loaded[u % NUB], 16 * (g * (NU // NUB) + u // NUB + 1))
                nc.scalar.activation(v, v, ACT.Identity, scale=col(outp, 0)
                                     ).then_inc(u_scaled, 1)

            def store_stream(g, u):
                (c, b, q), h = STREAM[u // 2], u % 2
                act.wait_ge(u_finished if u % 2 else u_added, NU // 2 * g + u // 2 + 1)
                act.dma_start(ov[chan(g, c), b][:, 2 * h:2 * h + 2, BW * q:BW * (q + 1)], ubuf[:, u % NUB, :, :]
                              ).then_inc(u_stored[u % NUB], 16)

            def stage(s, do_a, do_b, do_c):
                ga, gb, gc = s, s - 1, s - 2
                for n in range(NT):
                    if do_c:
                        for j in range(NPIECE):
                            if PIECES[j][0] == NT + n:
                                piece(gc, j)
                    if n + 2 < NT:
                        if do_b:
                            split_hi(gb, n + 2)
                    elif do_a:
                        split_hi(ga, n + 2 - NT)
                    if n + AHEAD < NT:
                        if do_b:
                            norm(gb, n + AHEAD)
                    elif do_a:
                        if n + AHEAD == NT:
                            act.wait_ge(gn1_ready, 2 * ga + 2)
                        norm(ga, n + AHEAD - NT)
                    if do_b:
                        for e, w in EDGES:
                            if e == n:
                                copy_edge(gb, e, w)
                        for j in range(NPIECE):
                            if PIECES[j][0] == n:
                                piece(gb, j)
                        for i, at in spill_pos.items():
                            if at == n:
                                spill(gb, i)
                    if do_a and n == STATS1[3]:
                        act.wait_ge(s1_root, s * 2 + 1)
                        nc.scalar.activation(t1[:, 6:7], t1[:, 5:6], ACT.Sqrt).then_inc(s1_root, 1)
                    if do_c:
                        if n == STATS2:
                            act.wait_ge(s2_root, gc * 2 + 1)
                            nc.scalar.activation(t2[:, 6:7], t2[:, 5:6], ACT.Sqrt).then_inc(s2_root, 1)
                            act.wait_ge(gn2_ready, gc + 1)
                        for c in range(CPG):
                            if n == BIAS_SHIFT[c]:
                                act.wait_ge(bias_loaded, 16 * (chan(gc, c) + 1))
                                nc.scalar.activation(bias[:, :], bias[:, :], ACT.Identity, bias=col(outp, 1)
                                                     ).then_inc(bias_shifted, 1)
                        for u in range(0, NU, 2):
                            if u_pos[u] == n:
                                scale_stream(gc, u)
                        for blk in KEPT:
                            if kept_pos[blk][1] + 1 == n:
                                store_kept(gc, blk)
                        for u in range(NU):
                            if min(u_pos[u] + 2, NT - 1) == n:
                                store_stream(gc, u)

            stages(act, stage)
            for blk in KEPT:
                act.wait_ge(kept_stored[blk], 16 * G)
            for i in range(NUB):
                act.wait_ge(u_stored[i], 16 * G * (NU // NUB))
            for s in x1_spilled.values():
                act.wait_ge(s, 16 * CH)

        @block.vector
        def _(dve):
            nc.vector.memset(zeros, 0.0).then_inc(zeros_ready, 1)
            dve.wait_ge(wall_loaded, 16)
            wv = wall.rearrange("p (c i) -> p c i", c=CH)
            hiw, low = squares[:, 0:CH], squares[:, CH:2 * CH]
            nc.vector.tensor_reduce(out=hiw, in_=wv, axis=AX.X, op=ALU.max).then_inc(scale_chain, 1)
            nc.vector.tensor_reduce(out=low, in_=wv, axis=AX.X, op=ALU.min).then_inc(scale_chain, 1)
            dve.wait_ge(scale_chain, 2)
            nc.vector.scalar_tensor_tensor(out=hiw, in0=low, scalar=-1.0, in1=hiw, op0=ALU.mult,
                                           op1=ALU.max).then_inc(scale_chain, 1)
            dve.wait_ge(scale_chain, 3)
            nc.vector.tensor_scalar(low, hiw, 1e-30, None, ALU.max).then_inc(scale_chain, 1)
            dve.wait_ge(scale_chain, 4)
            nc.vector.tensor_scalar(wsc[:, :, 1], low, 1.0 / WSCALE, None, ALU.mult).then_inc(scale_chain, 1)
            dve.wait_ge(scale_chain, 5)
            nc.vector.reciprocal(wsc[:, :, 0], wsc[:, :, 1]).then_inc(scale_chain, 1)
            dve.wait_ge(scale_chain, 6)
            nc.vector.memset(t1[:, 15:16], 0.0).then_inc(scale_chain, 1)

            def split_lo(g, n):
                N = NT * g + n
                dve.wait_ge(hi_ready, N + 1)
                nc.vector.tensor_tensor(XT[:, n % NB3, 1, :, 2:P + 2], psT[n % NB3][:, :, :],
                                        XT[:, n % NB3, 0, :, 2:P + 2], ALU.subtract).then_inc(lo_ready, 1)

            def evict(g, n):
                c, b, t = TILES[n]
                N = NT * g + n
                c0, c1 = (0 if t == 0 else PADC), min(TOUT, BW * (b + 1) - STEP * t)
                y = psY[n % NB3][:, :, c0:c1]
                xs = slot(c, b)[:, :, STEP * t + c0:STEP * t + c1]
                dve.wait_ge(convolved, N + 1)
                if n % NTC == 0:
                    dve.wait_ge(wback_ready, chan(g, c) + 1)
                if is_diag[n]:
                    nc.vector.tensor_tensor(y, y, mask_at(b, t, c0, c1), ALU.mult).then_inc(conv_masked, 1)
                    dve.wait_ge(conv_masked, ND * g + DIAG_BEFORE[n] + 1)
                nc.vector.scalar_tensor_tensor(out=xs, in0=y, scalar=col(wback, c), in1=xs,
                                               op0=ALU.mult, op1=ALU.add).then_inc(evicted, 1)

            def take_stats(half, src):
                c, b, q, h = half
                for k in range(2):
                    if q <= b:
                        e = ((c * (NBAND * (NBAND + 1) // 2) + b * (b + 1) // 2 + q) * K) + 2 * h + k
                    else:
                        up = sum(NBAND - 1 - bb for bb in range(b)) + q - b - 1
                        e = LO_ENTRIES + (c * UPPER_PER_CH + up) * K + 2 * h + k
                    last = nc.vector.bn_stats(entries[:, e, :], src[:, k, :])
                return last

            def stream_stats(g, a):
                uses = (NA - a % NAB + NAB - 1) // NAB
                dve.wait_ge(a_loaded[a % NAB], 16 * (g * uses + a // NAB + 1))
                take_stats(A_STREAM[a], abuf[:, a % NAB, :, :]).then_inc(a_done, 1)

            def early_stats(g, i):
                c, b, q, h = A_EARLY[i]
                if h == 0:
                    dve.wait_ge(x_loaded[(c, b, q)], 16 * (chan(g, c) + 1))
                take_stats(A_EARLY[i], transit[b][:, 2 * h:2 * h + 2, BW * q:BW * (q + 1)]).then_inc(early_done, 1)

            def inv_root(v, t, chain, base, root, g):
                dve.wait_ge(root, 2 * g + 2)
                nc.vector.reciprocal(t[:, 7:8], t[:, 6:7]).then_inc(chain, 1)
                dve.wait_ge(chain, base + 1)
                nc.vector.scalar_tensor_tensor(out=t[:, 8:9], in0=t[:, 7:8], scalar=t[:, 5:6], in1=t[:, 6:7],
                                               op0=ALU.mult, op1=ALU.add).then_inc(chain, 1)
                dve.wait_ge(chain, base + 2)
                nc.vector.tensor_scalar(t[:, 8:9], t[:, 8:9], 0.5, None, ALU.mult).then_inc(chain, 1)
                dve.wait_ge(chain, base + 3)
                nc.vector.reciprocal(t[:, 9:10], t[:, 8:9]).then_inc(chain, 1)
                dve.wait_ge(chain, base + 4)

            L1 = 11

            def stats1(g, part):
                base = g * L1
                if part == 0:
                    dve.wait_ge(a_done, NA * (g + 1))
                    dve.wait_ge(early_done, len(A_EARLY) * (g + 1))
                    nc.vector.memset(t1[:, 14:15], 0.0).then_inc(s1_chain, 1)
                    flat_e = entries[:, :, :].rearrange("p e s -> p (e s)")
                    nc.vector.bn_aggr(t1[:, 0:2], flat_e).then_inc(s1_chain, 1)
                    nc.vector.bn_aggr(nxt[:, 1:3], flat_e[:, LO_ENTRIES * 6:]).then_inc(s1_chain, 1)
                elif part == 1:
                    dve.wait_ge(s1_pool, 2 * g + 1)
                    nc.vector.tensor_scalar(col(nxt, 0), t1[:, 2:3], 1.0 / P, None, ALU.mult).then_inc(s1_chain, 1)
                    dve.wait_ge(s1_chain, base + 4)
                    nc.vector.tensor_tensor(t1[:, 10:11], t1[:, 0:1], col(nxt, 0), ALU.subtract
                                            ).then_inc(s1_chain, 1)
                    dve.wait_ge(s1_chain, base + 5)
                    nc.vector.scalar_tensor_tensor(out=t1[:, 3:4], in0=t1[:, 10:11], scalar=t1[:, 10:11],
                                                   in1=t1[:, 1:2], op0=ALU.mult, op1=ALU.add).then_inc(s1_chain, 1)
                elif part == 2:
                    dve.wait_ge(s1_pool, 2 * g + 2)
                    nc.vector.tensor_scalar(t1[:, 5:6], t1[:, 4:5], 1.0 / P, EPS, ALU.mult, ALU.add
                                            ).then_inc(s1_root, 1)
                else:
                    inv_root(g, t1, s1_chain, base + 6, s1_root, g)
                    nc.vector.scalar_tensor_tensor(out=t1[:, 11:12], in0=t1[:, 9:10], scalar=-1.0, in1=col(nxt, 0),
                                                   op0=ALU.mult, op1=ALU.mult).then_inc(s1_chain, 1)
                    dve.wait_ge(s1_chain, base + 11)

            def hand_over_norm(ga, gb):
                if gb is not None:
                    dve.wait_ge(diag_normed, ND * (gb + 1))
                nc.vector.tensor_copy(normp[:, 0:1], t1[:, 9:10]).then_inc(gn1_ready, 1)
                nc.vector.tensor_copy(normp[:, 1:2], t1[:, 11:12]).then_inc(gn1_ready, 1)

            def hand_over_sums(g):
                nc.vector.tensor_copy(cur[:, 0:3], nxt[:, :]).then_inc(cur_ready, 1)
                nc.vector.tensor_scalar(col(cur, 3), col(nxt, 0), -1.0, None, ALU.mult).then_inc(cur_ready, 1)

            NUP = float(CPG * UPPER_PER_CH * K * BW)
            L2 = 16

            def stats2(g):
                base = g * L2

                def link(i, ins):
                    ins.then_inc(s2_chain, 1)
                    dve.wait_ge(s2_chain, base + i)
                dve.wait_ge(pieces_done, NPIECE * (g + 1))
                wait(dve, u_scaled, NU // 2 * g)
                nc.vector.tensor_reduce(out=t2[:, 0:1], in_=sums[:, :], axis=AX.X, op=ALU.add).then_inc(s2_chain, 1)
                nc.vector.tensor_reduce(out=t2[:, 1:2], in_=squares[:, :], axis=AX.X, op=ALU.add
                                        ).then_inc(sums_read, 1)
                nc.vector.tensor_tensor(t2[:, 10:11], col(cur, 1), col(cur, 0), ALU.subtract).then_inc(s2_chain, 1)
                dve.wait_ge(s2_chain, base + 2)
                link(3, nc.vector.scalar_tensor_tensor(out=t2[:, 11:12], in0=t2[:, 10:11], scalar=t2[:, 10:11],
                                                       in1=col(cur, 2), op0=ALU.mult, op1=ALU.add))
                nc.vector.scalar_tensor_tensor(out=t2[:, 0:1], in0=col(cur, 1), scalar=NUP, in1=t2[:, 0:1],
                                               op0=ALU.mult, op1=ALU.add).then_inc(s2_chain, 1)
                dve.wait_ge(sums_read, g + 1)
                link(5, nc.vector.scalar_tensor_tensor(out=t2[:, 1:2], in0=t2[:, 11:12], scalar=NUP, in1=t2[:, 1:2],
                                                       op0=ALU.mult, op1=ALU.add))
                dve.wait_ge(s2_pool, g + 1)
                link(6, nc.vector.tensor_scalar(t2[:, 4:5], t2[:, 2:3], 1.0 / ROWN, None, ALU.mult))
                link(7, nc.vector.tensor_tensor(t2[:, 14:15], t2[:, 4:5], col(cur, 0), ALU.subtract))
                link(8, nc.vector.tensor_tensor(t2[:, 12:13], t2[:, 14:15], t2[:, 14:15], ALU.mult))
                link(9, nc.vector.scalar_tensor_tensor(out=t2[:, 13:14], in0=t2[:, 3:4], scalar=1.0 / ROWN,
                                                       in1=t2[:, 12:13], op0=ALU.mult, op1=ALU.subtract))
                nc.vector.tensor_scalar(t2[:, 5:6], t2[:, 13:14], 0.0, EPS, ALU.max, ALU.add).then_inc(s2_root, 1)
                inv_root(g, t2, s2_chain, base + 9, s2_root, g)
                link(14, nc.vector.tensor_scalar(col(outp, 0), t2[:, 9:10], 1.0, None, ALU.add))
                link(15, nc.vector.scalar_tensor_tensor(out=col(outp, 1), in0=t2[:, 9:10], scalar=-1.0,
                                                        in1=t2[:, 4:5], op0=ALU.mult, op1=ALU.mult))
                link(16, nc.vector.tensor_copy(t2[:, 15:16], t2[:, 9:10]))
                nc.vector.tensor_copy(t2[:, 15:16], t2[:, 9:10]).then_inc(gn2_ready, 1)

            def build_weights(g, c):
                sc = wsc[:, bass.ds(chan(g, c), 1), 0]
                dve.wait_ge(w_loaded, 16 * K * (chan(g, c) + 1))
                wait(dve, convolved, NT * g if c else NT * (g - 1) + NTC)
                if isinstance(g, int) and g == 0 and c == 0:
                    dve.wait_ge(scale_chain, 7)
                nc.vector.tensor_copy(col(wback, c), wsc[:, bass.ds(chan(g, c), 1), 1]).then_inc(wback_ready, 1)
                nc.vector.tensor_scalar(wsplit[:, c, 0, :, :], wstage[:, :, :], sc, None, ALU.mult
                                        ).then_inc(w_hi_built, 1)
                dve.wait_ge(w_hi_built, chan(g, c) + 1)
                nc.vector.scalar_tensor_tensor(out=wsplit[:, c, 1, :, :], in0=wstage[:, :, :], scalar=sc,
                                               in1=wsplit[:, c, 0, :, :], op0=ALU.mult, op1=ALU.subtract
                                               ).then_inc(w_built, 1)

            def finish_kept(g, blk, h):
                c, b, q = blk
                if h == 0:
                    dve.wait_ge(bias_shifted, chan(g, c) + 1)
                v = kept[(c, b)][:, 2 * h:2 * h + 2, BW * q:BW * (q + 1)]
                nc.vector.scalar_tensor_tensor(out=v, in0=v, scalar=col(outp, 0), in1=bias_at(b, q, h),
                                               op0=ALU.mult, op1=ALU.add).then_inc(kept_done, 1)

            def finish_stream(g, u):
                (c, b, q), h = STREAM[u // 2], u % 2
                dve.wait_ge(bias_shifted, chan(g, c) + 1)
                dve.wait_ge(u_loaded[u % NUB], 16 * (g * (NU // NUB) + u // NUB + 1))
                v = ubuf[:, u % NUB, :, :]
                nc.vector.scalar_tensor_tensor(out=v, in0=v, scalar=col(outp, 0), in1=bias_at(b, q, h),
                                               op0=ALU.mult, op1=ALU.add).then_inc(u_finished, 1)

            def stage(s, do_a, do_b, do_c):
                ga, gb, gc = s, s - 1, s - 2
                for n in range(NT):
                    if n + 2 < NT:
                        if do_b:
                            split_lo(gb, n + 2)
                    elif do_a:
                        split_lo(ga, n + 2 - NT)
                    if n >= 1:
                        if do_b:
                            evict(gb, n - 1)
                    elif do_c:
                        evict(gc, NT - 1)
                    if do_c:
                        if n == STATS2:
                            stats2(gc)
                        for blk in KEPT:
                            for h in range(2):
                                if kept_pos[blk][h] == n:
                                    finish_kept(gc, blk, h)
                        for u in range(1, NU, 2):
                            if u_pos[u] == n:
                                finish_stream(gc, u)
                    if do_a:
                        for a in range(NA):
                            if a_pos[a] == n:
                                stream_stats(ga, a)
                        if EARLY_STATS <= n < EARLY_STATS + len(A_EARLY):
                            early_stats(ga, n - EARLY_STATS)
                        if n in STATS1:
                            stats1(ga, STATS1.index(n))
                        if n == W_BUILD[0]:
                            build_weights(ga, 0)
                        if n == HAND_OVER_NORM:
                            hand_over_norm(ga, gb if do_b else None)
                    if do_b and n == HAND_OVER_SUMS:
                        hand_over_sums(gb)
                    if do_b and n == W_BUILD[1]:
                        build_weights(gb, 1)
            stages(dve, stage)

        @block.gpsimd
        def _(pool):
            nc.gpsimd.iota(pos_in, pattern=[[1, NPOS]], base=-(HH - 1), channel_multiplier=0,
                           allow_small_or_imprecise_dtypes=True).then_inc(pos_ready, 1)
            nc.gpsimd.memset(mask[:, :], 1.0).then_inc(const_ready, 1)
            nc.gpsimd.memset(ident[:, :], 0.0).then_inc(const_ready, 1)
            nc.gpsimd.memset(xn[:, :, :, :, :], 0.0).then_inc(const_ready, 1)
            nc.gpsimd.memset(wstage[:, :, :], 0.0).then_inc(const_ready, 1)
            pool.wait_ge(const_ready, 4)
            nc.gpsimd.affine_select(out=mask[:, :], in_=mask[:, :], pattern=[[1, MW]], compare_op=ALU.is_ge,
                                    fill=0.0, base=MLO, channel_multiplier=K).then_inc(const_ready, 1)
            nc.gpsimd.affine_select(out=ident[:, :], in_=ident[:, :], pattern=[[-1, P]], compare_op=ALU.not_equal,
                                    fill=1.0, base=0, channel_multiplier=1).then_inc(const_ready, 1)
            pool.wait_ge(const_ready, 6)

            def mask_tile(g, n):
                c, b, t = TILES[n]
                pool.wait_ge(diag_normed, ND * g + DIAG_BEFORE[n] + 1)
                v = xn[:, n % NB3, :, :, :]
                m = mask_at(b, t, 0, TIN)
                m = bass.AP(m.tensor, m.offset, [m.ap[0], [-XC, NPC], [1, K], [-1, XC]])
                nc.gpsimd.tensor_tensor(v, v, m, ALU.mult).then_inc(xn_ready, 1)

            def halo_from(g, n):
                c, b, t = TILES[n]
                N = NT * g + n
                if n % NTC == 0:
                    wait_alone(pool, halo_out, N)
                    nc.gpsimd.memset(halo[:, :, :, :, :], 0.0).then_inc(halo_zeroed, 1)
                    wait_alone(pool, halo_zeroed, chan(g, c) + 1)
                wait_alone(pool, convolved, N - NB3 + 1)
                for e, _ in EDGES:
                    if n > e and (c, t) == (TILES[e][0], TILES[e][2] + 1):
                        wait_alone(pool, edge_copied, 16 * K * (NEDGE * g + edges_before(n)))
                nc.gpsimd.tensor_copy(XT[:, n % NB3, :, :, 0:2], halo[:, t, :, :, :]).then_inc(halo_in, 1)

            def halo_to(g, n):
                c, b, t = TILES[n]
                N = NT * g + n
                wait_alone(pool, halo_in, N + 1)
                wait_alone(pool, lo_ready, N + 1)
                nc.gpsimd.tensor_copy(halo[:, t, :, :, :], XT[:, n % NB3, :, :, P:P + 2]).then_inc(halo_out, 1)

            def add_bias(g, u):
                (c, b, q), h = STREAM[u // 2], u % 2
                if u % (NU // CPG) == 0:
                    wait_alone(pool, bias_shifted, chan(g, c) + 1)
                pool.wait_ge(u_scaled, NU // 2 * g + u // 2 + 1)
                v = ubuf[:, u % NUB, :, :]
                nc.gpsimd.tensor_tensor(v, v, bias_at(b, q, h), ALU.add).then_inc(u_added, 1)

            def stage(s, do_a, do_b, do_c):
                ga, gb, gc = s, s - 1, s - 2
                for n in range(NT):
                    if n + AHEAD < NT:
                        if do_b and is_diag[n + AHEAD]:
                            mask_tile(gb, n + AHEAD)
                    elif do_a and is_diag[n + AHEAD - NT]:
                        mask_tile(ga, n + AHEAD - NT)
                    if n + 1 < NT:
                        if do_b:
                            halo_to(gb, n + 1)
                    elif do_a:
                        halo_to(ga, 0)
                    if n + 2 < NT:
                        if do_b:
                            halo_from(gb, n + 2)
                    elif do_a:
                        halo_from(ga, n + 2 - NT)
                    if do_a and n == STATS1[0]:
                        wait_alone(pool, s1_chain, 11 * ga + 3)
                        nc.gpsimd.partition_all_reduce(t1[:, 2:3], t1[:, 0:1], P, RED.add).then_inc(s1_pool, 1)
                    if do_a and n == STATS1[1]:
                        wait_alone(pool, s1_chain, 11 * ga + 6)
                        nc.gpsimd.partition_all_reduce(t1[:, 4:5], t1[:, 3:4], P, RED.add).then_inc(s1_pool, 1)
                    if do_c:
                        if n == STATS2:
                            wait_alone(pool, s2_chain, 16 * gc + 5)
                            nc.gpsimd.partition_all_reduce(t2[:, 2:4], t2[:, 0:2], P, RED.add).then_inc(s2_pool, 1)
                        for u in range(NU):
                            if u_pos[u] == n and u % 2 == 0:
                                add_bias(gc, u)

            stages(pool, stage)

        @block.tensor
        def _(pe):
            pe.wait_ge(small_loaded, 96)
            pe.wait_ge(h1_ready, 1)
            for j in range(NPOS // BW):
                cols = slice(j * BW, (j + 1) * BW)
                if j >= 2:
                    pe.wait_ge(h2_ready, j - 1)
                nc.tensor.matmul(psT[j % 2][0:DIM, :, :].rearrange("p a b -> p (a b)"), w2s[:, :], h1[:, cols],
                                 start=True, stop=True).then_inc(mlp2_done, 1)
                pe.wait_ge(h2_ready, j + 1)
                if j >= 2:
                    pe.wait_ge(table_ready, j - 1)
                nc.tensor.matmul(psY[j % 2][0:CH, :, :].rearrange("p a b -> p (a b)"), w3s[:, :], h2[:, cols],
                                 start=True, stop=True).then_inc(mlp3_done, 1)
            pe.wait_ge(table_ready, 8)
            pe.wait_ge(const_ready, 6)

            def transpose(N, m):
                wait(pe, lo_ready, N - NB3 + 1)
                pe.wait_ge(xn_ready, N + 1)
                for i in range(NPC):
                    last = nc.tensor.transpose(psT[m][:, i, :], xn[:, m, i, :, :].rearrange("p k c -> p (k c)"), ident[:, :])
                last.then_inc(transposed, 1)

            def convolve(N, m, c):
                pe.wait_ge(lo_ready, N + 1)
                pe.wait_ge(halo_in, N + 1)
                wait(pe, evicted, N - NB3 + 1)
                products = [(i, sh, xp, wp) for i in range(NPC) for sh in range(3)
                            for xp, wp in ((0, 0), (0, 1), (1, 0))]
                for j, (i, sh, xp, wp) in enumerate(products):
                    lo_c = max(0, PADC - XC * i)
                    hi_c = min(WC, TOUT + PADC - XC * i)
                    rows = min(K, NE - K * sh)
                    o = XC * i - PADC
                    last = nc.tensor.matmul(psY[m][:, 0:rows, o + lo_c:o + hi_c],
                                            XT[:, m, xp, i, 2 - sh:2 - sh + P],
                                            wsplit[:, c, wp, K * sh:K * sh + rows, lo_c:hi_c],
                                            start=(j == 0), stop=(j == len(products) - 1), skip_group_check=True)
                last.then_inc(convolved, 1)

            def triple(N, c, ahead=NB3):
                for i in range(NB3):
                    if i < ahead:
                        transpose(N + i + 2, (i + 2) % NB3)
                    convolve(N + i, i, c)

            def group(g):
                first = NT * g
                pe.wait_ge(w_built, chan(g, 0) + 1)
                triple(first, 0)
                with pe.Fori(1, NTC // NB3) as j:
                    triple(first + NB3 * j, 0)
                pe.wait_ge(w_built, chan(g, 1) + 1)
                triple(first + NTC, 1)
                with pe.Fori(NTC // NB3 + 1, 2 * NTC // NB3 - 1) as j:
                    triple(first + NB3 * j, 1)

            transpose(0, 0)
            transpose(1, 1)
            group(0)
            with pe.Fori(1, G) as g:
                triple(NT * g - NB3, 1)
                group(g)
            triple(NT * G - NB3, 1, 1)


_INS = ["x", "w", "w1", "b1", "w2", "b2", "w3", "b3"]


def kernel(x, L0_conv_weight, L1_conv_W1, L1_conv_b1, L1_conv_W2, L1_conv_b2, L1_conv_W3, L1_conv_b3):
    import numpy as _np
    import concourse.bacc as _bacc
    from concourse import mybir as _mybir
    from concourse.bass_utils import run_bass_kernel_spmd as _run

    nc = _bacc.Bacc("TRN2", target_bir_lowering=False, num_devices=1)
    values = [x, _np.asarray(L0_conv_weight)[:, ::-1, ::-1], L1_conv_W1, L1_conv_b1, L1_conv_W2, L1_conv_b2,
              L1_conv_W3, L1_conv_b3]
    arrays, args = {}, []
    for name, v in zip(_INS, values):
        a = _np.ascontiguousarray(v)
        arrays[f"in_{name}"] = a
        args.append(nc.dram_tensor(f"in_{name}", a.shape, _mybir.dt.from_np(a.dtype), kind="ExternalInput").ap())
    out = nc.dram_tensor("out_0", x.shape, _mybir.dt.float32, kind="ExternalOutput").ap()
    preact_conv_kernel(nc, *args, out)
    r = _run(nc, [arrays], core_ids=[0])
    return r.results[0]["out_0"]
```

```python
import concourse.bass as bass
from concourse import mybir
from contextlib import ExitStack


def preact_conv_kernel(nc, x, wflip, w1, b1, w2, b2, w3, b3, out):
    f32, f16, bf16 = mybir.dt.float32, mybir.dt.float16, mybir.dt.bfloat16
    ALU = mybir.AluOpType
    ACT = mybir.ActivationFunctionType
    AX = mybir.AxisListType
    RED = bass.bass_isa.ReduceOp

    _, CH, HH, WW = x.shape
    _, TR, TS = wflip.shape
    DIM = w2.shape[0]
    P, K, BW = 128, 4, 512
    CPG = 2
    G = CH // CPG
    NBAND = HH // (P * K)
    XC = P // K
    NPC = 4
    TIN = NPC * XC
    PADC = TS // 2
    TOUT = TIN - PADC
    STEP = TIN - 2 * PADC
    WC = XC + TS - 1
    NE = TR + K - 1
    ROWN = CPG * HH * WW
    EPS = 1e-5
    WSCALE = 256.0
    NB3 = 3
    AHEAD = 4

    def band_tiles(b):
        return -(-(BW * (b + 1) - TOUT) // STEP) + 1
    TILES = [(c, b, t) for c in range(CPG) for b in range(NBAND) for t in range(band_tiles(b))]
    NT = len(TILES)
    NTC = NT // CPG
    MAXT = band_tiles(NBAND - 1)
    is_diag = [STEP * t + TIN > BW * b for c, b, t in TILES]
    DIAG_BEFORE = [sum(is_diag[:n]) for n in range(NT + 1)]
    ND = DIAG_BEFORE[NT]

    EDGES = [(n, BW * (b + 1) - STEP * (t + 1)) for n, (c, b, t) in enumerate(TILES)
             if b < NBAND - 1 and t == band_tiles(b) - 1 and BW * (b + 1) > STEP * (t + 1)]
    assert all(w <= XC - STEP % XC for _, w in EDGES)
    edges_before = lambda n: sum(e < n for e, _ in EDGES)
    NEDGE = len(EDGES)

    LOWER = [(c, b, q) for c in range(CPG) for b in range(NBAND) for q in range(b + 1)]
    NL = len(LOWER)
    first_tile = {blk: next(n for n, (c, b, t) in enumerate(TILES)
                            if (c, b) == blk[:2] and STEP * t + TIN > BW * blk[2]) for blk in LOWER}
    last_tile = {blk: next(n for n, (c, b, t) in enumerate(TILES)
                           if (c, b) == blk[:2] and STEP * t + TOUT >= BW * (blk[2] + 1)) for blk in LOWER}
    KEPT = [blk for blk in LOWER if blk[1] >= 2]
    STREAM = [(c, b, q) for c in range(CPG) for b in range(NBAND) for q in range(NBAND)
              if (c, b, q) not in KEPT]
    NU = 2 * len(STREAM)
    NR = 2 * len(KEPT)
    A_HALVES = [(c, b, q, h) for c in range(CPG) for b in range(NBAND) for q in range(NBAND) for h in range(2)]
    A_EARLY = [x for x in A_HALVES if x[0] == 0 and x[1] < 2 and x[2] <= x[1]]
    A_STREAM = [x for x in A_HALVES if x not in A_EARLY]
    NA = len(A_STREAM)
    NAB, NUB = 4, 4
    UPPER_PER_CH = NBAND * (NBAND - 1) // 2
    LO_ENTRIES = CPG * (NBAND * NBAND - UPPER_PER_CH) * K

    BIAS_LOAD, BIAS_SHIFT = {1: 43}, {0: 4, 1: 46}
    U_WINDOW = ((5, 41), (47, 87))
    A_END = 82
    U_WEIGHT = lambda n: 1.8 if n < 10 else 1.5 if n > 82 else 1.0
    A_FIRST = ((-6, -4), (-6, -3), (-5, -3), (-5, -2), (-3, -1), (-2, 0), (-2, 1), (-1, 2))
    A_WEIGHT = lambda n: 1.5 if n < 3 else 0.8 if 4 < n < 10 else 1.1 if n > 60 else 1.0
    U_ON_DVE = lambda n, u: n > 85 or (u % 2 == 1 if n > 78 or 36 < n < 42 else u % 4 == 3)
    NEXT_BIAS_LOAD = 89
    TRANSIT_LOAD = {1: {(0, 0): 24, (1, 0): 31, (1, 1): 37}, 0: {(0, 0): 54, (1, 0): 59, (1, 1): 63}}
    EARLY_STATS = (60, 62, 65, 67, 70, 72)
    W_LOAD, W_BUILD = {1: 10, 0: 55}, {1: 20, 0: 65}
    STATS1, HAND_OVER_NORM, STATS2, HAND_OVER_SUMS = (83, 84, 85, 85), 85, (2, 3, 4), 5
    parts = [(i, 0, BW, last_tile[blk]) for i, blk in enumerate(LOWER)]
    split = STEP * (MAXT - 3) + TOUT - BW * (NBAND - 1)
    parts[-1:] = [(NL - 1, 0, split, NT - 3), (NL - 1, split, BW, NT - 1)]
    PIECES = []
    at, used = 0, 0
    for i, c0, c1, done in parts:
        nr = 1 if 2 * (c1 - c0) > BW else 2
        for r in range(0, K, nr):
            if done + 2 > at:
                at, used = done + 2, 0
            elif used == 2:
                at, used = at + 1, 0
            used += 1
            PIECES.append((at, i, r, nr, c0, c1, done))
    NPIECE = len(PIECES)
    piece_end = {i: max(j for j, x in enumerate(PIECES) if x[1] == i) + 1 for i in range(NL)}
    spill_pos = {i: last_tile[LOWER[i]] + 2 for i in range(NL) if LOWER[i][1] < 2}

    KEPT_RELOAD = 3
    KEPT_LEAD = 15
    kept_pos = {}
    for c in range(CPG):
        at = (STATS2[2] + 1, BIAS_SHIFT[1] + 1)[c]
        for blk in KEPT:
            if blk[0] == c:
                at = max(at, first_tile[blk] - KEPT_LEAD)
                hurry = first_tile[blk] - AHEAD - at < 7
                kept_pos[blk] = (at, at if hurry else at + 1)
                at = kept_pos[blk][1] + 1

    def a_items(p, positions, s, n, do_next):
        now = [(s, a) for a in range(len(positions))
               if positions[a] == n or (isinstance(s, int) and s == 0 and n == 0 and positions[a] < 0)]
        first = [load if positions is p.a_load else use for load, use in A_FIRST]
        return now + [(s + 1, a) for a, at in enumerate(first) if do_next and at == n - NT]

    def plan(do_a, do_b, do_c, on_dve=None):
        traffic = [0.0] * (NT + 8)

        def book(at, megabytes, over=2):
            for i in range(over):
                traffic[at + i] += megabytes / over
        for blk in KEPT:
            if do_c:
                book(kept_pos[blk][1] + 1, 1.0)
            if do_b:
                book(kept_pos[blk][1] + KEPT_RELOAD, 1.0)
        for at in spill_pos.values():
            book(at, 1.0 * do_b)
        for c, of in TRANSIT_LOAD.items():
            for at in of.values():
                book(at, 1.0 * (do_b if c else do_a))
        book(BIAS_LOAD[1], 1.8 * do_c)
        book(NEXT_BIAS_LOAD, 1.8 * do_b)

        def spread(count, megabytes, lo, hi, weight):
            smooth = {n: sum(traffic[max(0, n - 1):n + 2]) / len(traffic[max(0, n - 1):n + 2])
                      for n in range(lo, hi + 1)}

            def room(n):
                return max(0.02, level * weight(n) - smooth[n])
            level = 0.0
            while sum(room(n) for n in smooth) < count * megabytes:
                level += 0.01
            at, acc, n = [], room(lo), lo
            for i in range(count):
                while acc < (i + 0.5) * megabytes and n < hi:
                    n += 1
                    acc += room(n)
                at.append(n)
            return at
        p = Plan()
        p.u_load, p.u, p.on_dve, p.u_store, p.a_load, p.a = [], [], [], [], [], []
        if do_c:
            for c, (lo, hi) in enumerate(U_WINDOW):
                for at in spread(NU // 2, 1.0, lo, hi, U_WEIGHT if do_a else lambda n: 1.0):
                    u = len(p.u)
                    p.u_load.append(max(at - 2, p.u_store[u - NUB] + 1) if u >= NUB else 0)
                    p.u.append(min(max(at, p.u_load[u] + 1, p.u[-1] if u else 0), hi))
                    p.on_dve.append(on_dve[u] if on_dve else U_ON_DVE(p.u[u], u))
                    p.u_store.append(min(p.u[u] + (1 if p.on_dve[u] else 2), NT - 1))
                    book(p.u_load[u], 0.5, 1)
                    book(p.u_store[u], 0.5, 1)
        if do_a:
            for at in spread(NA, 0.5, 0, A_END - 2, A_WEIGHT if do_c else lambda n: 1.0):
                a = len(p.a)
                if a < len(A_FIRST):
                    load, use = A_FIRST[a]
                else:
                    load = max(at, p.a[a - NAB] + 1)
                    use = min(load + 2, A_END)
                p.a_load.append(load)
                p.a.append(use)
        return p

    class Plan:
        pass
    STEADY = plan(True, True, True)
    on_dve = STEADY.on_dve
    u_before = [[sum(v == d for v in on_dve[:u]) for u in range(NU + 1)] for d in (False, True)]
    N_DVE, N_POOL = u_before[1][NU], u_before[0][NU]

    xv = x.rearrange("o c (b p k) w -> (o c) b p k w", p=P, k=K)
    ov = out.rearrange("o c (b p k) w -> (o c) b p k w", p=P, k=K)
    taps_dram = nc.dram_tensor("taps_scratch", [CH * TR, XC * WC], f32, kind="Internal").ap()
    taps_v = taps_dram.rearrange("(c r) (p j) -> c p r j", r=TR, j=WC)
    NPOS = 2 * HH
    bias_dram = nc.dram_tensor("bias_scratch", [CH, NPOS], f32, kind="Internal").ap()
    VLO = -(WW - 1)
    NV = BW * (NBAND - 1) + K - 1 - VLO + 1

    ctx = ExitStack()
    with ctx:
        def sb(name, shape, dt):
            return ctx.enter_context(nc.sbuf_tensor(name, shape, dt))

        def sem(name):
            return ctx.enter_context(nc.semaphore(name))

        transit = {b: sb(f"band{b}", [P, K, BW * (b + 1)], f32) for b in (0, 1)}
        kept = {(c, b): sb(f"kept_c{c}_band{b}", [P, K, BW * (b + 1)], f32)
                for c in range(CPG) for b in (2, 3)}

        def slot(c, b):
            return transit[b] if b < 2 else kept[(c, b)]

        bias = sb("bias", [P, NV], f32)
        abuf = sb("abuf", [P, NAB, 2, BW], f32)
        ubuf = sb("ubuf", [P, NUB, 2, BW], f32)
        xn = sb("xn", [P, NB3, NPC, K, XC], f32)
        XT = sb("XT", [P, NB3, 2, NPC, P + 2], f16)
        halo = sb("halo", [P, MAXT, 2, NPC, 2], f16)
        wstage = sb("wstage", [P, NE, WC], f32)
        wsplit = sb("wsplit", [P, CPG, 2, NE, WC], f16)
        MLO = -STEP * (band_tiles(0) - 1) - (TIN - 1)
        MW = 728
        mask = sb("mask", [P, MW], bf16)
        ident = sb("ident", [P, P], f32)
        entries = sb("entries", [P, 2 * len(A_HALVES), 6], f32)
        nxt = sb("nxt", [P, 3], f32)
        normp = sb("normp", [P, 2], f32)
        cur = sb("cur", [P, 4], f32)
        outp = sb("outp", [P, 2], f32)
        wback = sb("wback", [P, CPG], f32)

        def col(t, i):
            return t[:, i:i + 1]
        wsc = sb("wsc", [P, CH, 2], f32)
        sums = sb("sums", [P, NT], f32)
        squares = sb("squares", [P, NPIECE], f32)
        t1 = sb("t1", [P, 16], f32)
        t2 = sb("t2", [P, 16], f32)
        small = sb("small", [DIM, 8], f32)
        w2s = sb("w2s", [DIM, DIM], f32)
        w3s = sb("w3s", [DIM, CH], f32)
        psT = [ctx.enter_context(nc.psum_tensor(f"psT{i}", [P, NPC, P], f32)) for i in range(NB3)]
        psY = [ctx.enter_context(nc.psum_tensor(f"psY{i}", [P, K, TIN], f32)) for i in range(NB3)]
        junk = ctx.enter_context(nc.psum_tensor("junk", [P, BW], f32))

        def flat(t):
            return t[:, :, :].rearrange("p a b -> p (a b)")
        pos_in = flat(kept[(0, 3)])[0:DIM, 0:NPOS]
        h1 = flat(kept[(0, 3)])[0:DIM, NPOS:2 * NPOS]
        h2 = flat(kept[(1, 3)])[0:DIM, 0:NPOS]
        table = flat(kept[(1, 3)])[0:CH, NPOS:2 * NPOS]
        zeros = flat(kept[(0, 2)])[0:CH * TR, 0:XC * WC]
        wall = flat(kept[(1, 2)])[:, 0:CH * TR * TS]

        const_ready = sem("const_ready")
        small_loaded = sem("small_loaded")
        wall_loaded = sem("wall_loaded")
        zeros_ready = sem("zeros_ready")
        taps_zeroed = sem("taps_zeroed")
        taps_stored = sem("taps_stored")
        pos_ready = sem("pos_ready")
        h1_ready = sem("h1_ready")
        mlp2_done = sem("mlp2_done")
        h2_ready = sem("h2_ready")
        mlp3_done = sem("mlp3_done")
        table_ready = sem("table_ready")
        table_stored = sem("table_stored")
        scale_chain = sem("scale_chain")
        a_loaded = [sem(f"a_loaded{i}") for i in range(NAB)]
        a_done = sem("a_done")
        early_done = sem("early_done")
        x_loaded = {}
        for c, b, q in LOWER:
            x_loaded[(c, b, q)] = sem(f"x_loaded_{c}{b}{q}") if b >= 2 or c == 0 else x_loaded[(0, b, q)]
        x1_spilled = {(b, q): sem(f"x1_spilled_{b}{q}") for b in (0, 1) for q in range(b + 1)}
        kept_stored = {blk: sem("kept_stored_%d%d%d" % blk) for blk in KEPT}
        u_loaded = [sem(f"u_loaded{i}") for i in range(NUB)]
        u_scaled = sem("u_scaled")
        u_added = sem("u_added")
        u_finished = sem("u_finished")
        u_stored = [sem(f"u_stored{i}") for i in range(NUB)]
        kept_done = sem("kept_done")
        bias_loaded = sem("bias_loaded")
        bias_shifted = sem("bias_shifted")
        w_loaded = sem("w_loaded")
        w_built = sem("w_built")
        w_hi_built = sem("w_hi_built")
        wback_ready = sem("wback_ready")
        diag_normed = sem("diag_normed")
        xn_ready = sem("xn_ready")
        transposed = sem("transposed")
        hi_ready = sem("hi_ready")
        lo_ready = sem("lo_ready")
        halo_zeroed = sem("halo_zeroed")
        halo_in = sem("halo_in")
        halo_out = sem("halo_out")
        edge_copied = sem("edge_copied")
        convolved = sem("convolved")
        conv_masked = sem("conv_masked")
        evicted = sem("evicted")
        pieces_done = sem("pieces_done")
        tiles_summed = sem("tiles_summed")
        squares_read = sem("squares_read")
        s1_chain = sem("s1_chain")
        s1_pool = sem("s1_pool")
        s1_root = sem("s1_root")
        s2_chain = sem("s2_chain")
        s2_pool = sem("s2_pool")
        s2_root = sem("s2_root")
        gn1_ready = sem("gn1_ready")
        cur_ready = sem("cur_ready")
        gn2_ready = sem("gn2_ready")

        def chan(g, c):
            return CPG * g + c

        def wait(eng, s, value):
            if not isinstance(value, int) or value > 0:
                eng.wait_ge(s, value)

        def wait_alone(eng, s, value):
            if not isinstance(value, int) or value > 0:
                eng.wait_ge(s, value)
                eng.nop(nofuse=True)

        def bias_at(b, q, h):
            start = 2 * h + BW * b - BW * q - VLO
            full = bias[:, :]
            return bass.AP(full.tensor, start, [[full.ap[0][0], P], [1, 2], [-1, BW]])

        def out_columns(b, t):
            return (0 if t == 0 else PADC), min(TOUT, BW * (b + 1) - STEP * t)

        def mask_at(b, t, c0, c1):
            start = BW * b - STEP * t - c0 - MLO
            full = mask[:, :]
            return bass.AP(full.tensor, start, [[full.ap[0][0], P], [1, K], [-1, c1 - c0]])

        block = ctx.enter_context(nc.Block())

        def stages(eng, stage):
            stage(0, True, False, False, True)
            stage(1, True, True, False, True)
            with eng.Fori(2, G - 1) as s:
                stage(s, True, True, True, True)
            stage(G - 1, True, True, True, False)
            stage(G, False, True, True, False)
            stage(G + 1, False, False, True, False)

        @block.sync
        def _(sp):
            sp.dma_start(small[:, 0:1], w1.rearrange("o d -> d o")).then_inc(small_loaded, 16)
            sp.dma_start(small[:, 1:2], b1.rearrange("(d o) -> d o", o=1)).then_inc(small_loaded, 16)
            sp.dma_start(small[:, 2:3], b2.rearrange("(d o) -> d o", o=1)).then_inc(small_loaded, 16)
            sp.dma_start(small[0:CH, 3:4], b3.rearrange("(d o) -> d o", o=1)).then_inc(small_loaded, 16)
            sp.dma_start(w2s[:, :], w2).then_inc(small_loaded, 16)
            sp.dma_start(w3s[:, :], w3).then_inc(small_loaded, 16)
            wf = wflip.rearrange("c r s -> (c r s)")
            sp.dma_start(wall, wf.partition_broadcast(P)).then_inc(wall_loaded, 16)
            sp.wait_ge(zeros_ready, 1)
            sp.dma_start(taps_dram[:, :], zeros).then_inc(taps_zeroed, 16)
            sp.wait_ge(taps_zeroed, 16)
            sp.dma_start(bass.AP(taps_dram.tensor, 0, [[XC * WC, CH * TR], [WC + 1, XC], [1, TS]]),
                         bass.AP(wflip.tensor, 0, [[TS, CH * TR], [0, XC], [1, TS]])).then_inc(taps_stored, 16)

            def stage(s, do_a, do_b, do_c, do_next):
                p, ga, gb, gc = plan(do_a, do_b, do_c, on_dve), s, s - 1, s - 2
                if isinstance(s, int) and s == 1:
                    sp.wait_ge(table_ready, 8)
                    sp.dma_start(bias_dram[:, :], table).then_inc(table_stored, 16)
                    sp.wait_ge(table_stored, 16)
                    sp.wait_ge(scale_chain, 6)
                for n in range(NT):
                    for g, a in a_items(p, p.a_load, s, n, do_next):
                        c, b, q, h = A_STREAM[a]
                        wait_alone(sp, a_done, g * NA + (a - NAB + 1 if a >= NAB else 0))
                        sp.dma_start(abuf[:, a % NAB, :, :],
                                     xv[chan(g, c), b][:, 2 * h:2 * h + 2, BW * q:BW * (q + 1)]
                                     ).then_inc(a_loaded[a % NAB], 16)
                    if do_b:
                        load_transit(gb, 1, n)
                        for blk in KEPT:
                            if kept_pos[blk][1] + KEPT_RELOAD == n:
                                c, b, q = blk
                                wait_alone(sp, kept_stored[blk], 16 * gb)
                                sp.dma_start(kept[(c, b)][:, :, BW * q:BW * (q + 1)],
                                             xv[chan(gb, c), b][:, :, BW * q:BW * (q + 1)]
                                             ).then_inc(x_loaded[blk], 16)
                        if n == W_LOAD[1]:
                            load_taps(gb, 1)
                    if do_a and n == W_LOAD[0]:
                        load_taps(ga, 0)
                    if do_a:
                        load_transit(ga, 0, n)
                    if do_c:
                        for u in range(NU):
                            if p.u_load[u] == n:
                                (c, b, q), h = STREAM[u // 2], u % 2
                                wait_alone(sp, u_stored[u % NUB], 16 * (gc * (NU // NUB) + u // NUB))
                                spilled = q <= b
                                if spilled:
                                    wait_alone(sp, x1_spilled[(b, q)], 16 * (chan(gc, c) + 1))
                                src = (ov if spilled else xv)[chan(gc, c), b]
                                sp.dma_start(ubuf[:, u % NUB, :, :], src[:, 2 * h:2 * h + 2, BW * q:BW * (q + 1)]
                                             ).then_inc(u_loaded[u % NUB], 16)
                        if n == BIAS_LOAD[1]:
                            load_bias(gc, 1)
                    if do_b and n == NEXT_BIAS_LOAD:
                        load_bias(gb, 0)

            def load_transit(g, c, n):
                for (b, q), at in TRANSIT_LOAD[c].items():
                    if at == n:
                        wait_alone(sp, x1_spilled[(b, q)], 16 * chan(g, c))
                        i = LOWER.index((1 - c, b, q))
                        wait_alone(sp, pieces_done, NPIECE * (g - 1 + c) + piece_end[i] if c or not isinstance(g, int) or g else 0)
                        sp.dma_start(transit[b][:, :, BW * q:BW * (q + 1)],
                                     xv[chan(g, c), b][:, :, BW * q:BW * (q + 1)]
                                     ).then_inc(x_loaded[(c, b, q)], 16)

            def load_taps(g, c):
                sp.wait_ge(taps_stored, 16)
                wait_alone(sp, w_built, chan(g, c))
                if isinstance(g, int) and g == 0 and c == 0:
                    sp.wait_ge(const_ready, 6)
                for k in range(K):
                    sp.dma_start(wstage[XC * k:XC * (k + 1), k:k + TR, :], taps_v[chan(g, c)]
                                 ).then_inc(w_loaded, 16)

            def load_bias(g, c):
                wait_alone(sp, kept_done, g * NR + c * (NR // 2))
                for done, of in ((u_added, u_before[0]), (u_finished, u_before[1])):
                    wait_alone(sp, done, g * of[NU] + c * of[NU // 2])
                row = bias_dram[bass.ds(chan(g, c), 1), :]
                src = bass.AP(row.tensor, row.offset, [[K, P], [1, NV]])
                sp.dma_start(bias[:, :], src).then_inc(bias_loaded, 16)

            stages(sp, stage)

        @block.scalar
        def _(act):
            act.wait_ge(small_loaded, 96)
            act.wait_ge(pos_ready, 1)
            act.wait_ge(const_ready, 6)
            nc.scalar.activation(h1, pos_in, ACT.Relu, bias=small[:, 1:2], scale=small[:, 0:1]).then_inc(h1_ready, 1)
            for j in range(NPOS // BW):
                cols = slice(j * BW, (j + 1) * BW)
                act.wait_ge(mlp2_done, j + 1)
                nc.scalar.activation(h2[:, cols], psT[j % 2][0:DIM, :, :].rearrange("p a b -> p (a b)"),
                                     ACT.Relu, bias=small[:, 2:3]).then_inc(h2_ready, 1)
                act.wait_ge(mlp3_done, j + 1)
                nc.scalar.activation(table[:, cols], psY[j % 2][0:CH, :, :].rearrange("p a b -> p (a b)"),
                                     ACT.Identity, bias=small[0:CH, 3:4]).then_inc(table_ready, 1)

            def norm(g, n):
                c, b, t = TILES[n]
                N = NT * g + n
                for q in range(b + 1):
                    if first_tile[(c, b, q)] == n:
                        act.wait_ge(x_loaded[(c, b, q)], 16 * (g + 1) if b >= 2 else 16 * (chan(g, c) + 1))
                wait(act, transposed, N - NB3 + 1)
                if n > 0 and is_diag[n - 1] and not is_diag[n]:
                    act.wait_ge(xn_ready, N)
                width = min(TIN, BW * (b + 1) - STEP * t)
                whole, rest = divmod(width, XC)
                to = xn[:, n % NB3, :, :, :].rearrange("p i k c -> p k i c")
                x0 = STEP * t
                last = nc.scalar.activation(to[:, :, 0:whole, :], slot(c, b)[:, :, x0:x0 + XC * whole].rearrange(
                    "p k (i c) -> p k i c", c=XC), ACT.Identity, bias=col(normp, 1), scale=col(normp, 0))
                if rest:
                    last = nc.scalar.activation(to[:, :, whole, 0:rest], slot(c, b)[:, :, x0 + XC * whole:x0 + width],
                                                ACT.Identity, bias=col(normp, 1), scale=col(normp, 0))
                last.then_inc(diag_normed if is_diag[n] else xn_ready, 1)

            def split_hi(g, n):
                N = NT * g + n
                act.wait_ge(transposed, N + 1)
                wait(act, convolved, N - NB3 + 1)
                wait(act, halo_out, N - NB3 + 1)
                for e, _ in EDGES:
                    if n == e + NB3:
                        act.wait_ge(edge_copied, 16 * K * (NEDGE * g + edges_before(n)))
                nc.scalar.copy(XT[:, n % NB3, 0, :, 2:P + 2], psT[n % NB3][:, :, :]).then_inc(hi_ready, 1)

            def copy_edge(g, n, w):
                c, b, t = TILES[n]
                act.wait_ge(lo_ready, NT * g + n + 1)
                act.wait_ge(halo_zeroed, chan(g, c) + 1)
                piece_i, col = divmod(STEP, XC)
                for k in range(K):
                    act.dma_start(halo[XC * k:XC * k + w, t + 1, :, 0, :],
                                  XT[XC * k + col:XC * k + col + w, n % NB3, :, piece_i, P:P + 2]
                                  ).then_inc(edge_copied, 16)

            def piece(g, j):
                _, i, r, nr, c0, c1, done = PIECES[j]
                c, b, q = LOWER[i]
                act.wait_ge(evicted, NT * g + done + 1)
                if j == 0:
                    act.wait_ge(cur_ready, 2 * g + 2)
                    wait(act, squares_read, g)
                wait(act, pieces_done, NPIECE * g + j)
                nc.scalar.activation(junk[:, 0:nr * (c1 - c0)].rearrange("p (r c) -> p r c", r=nr),
                                     slot(c, b)[:, r:r + nr, BW * q + c0:BW * q + c1], ACT.Square,
                                     bias=col(cur, 3), accum_out=squares[:, j:j + 1]).then_inc(pieces_done, 1)

            def spill(g, i):
                c, b, q = LOWER[i]
                act.wait_ge(evicted, NT * g + last_tile[LOWER[i]] + 1)
                act.dma_start(ov[chan(g, c), b][:, :, BW * q:BW * (q + 1)], transit[b][:, :, BW * q:BW * (q + 1)]
                              ).then_inc(x1_spilled[(b, q)], 16)

            def store_kept(g, blk):
                c, b, q = blk
                i = KEPT.index(blk)
                act.wait_ge(kept_done, NR * g + 2 * i + 2)
                act.dma_start(ov[chan(g, c), b][:, :, BW * q:BW * (q + 1)], kept[(c, b)][:, :, BW * q:BW * (q + 1)]
                              ).then_inc(kept_stored[blk], 16)

            def scale_stream(g, u):
                c, b, q = STREAM[u // 2]
                v = ubuf[:, u % NUB, :, :]
                act.wait_ge(u_loaded[u % NUB], 16 * (g * (NU // NUB) + u // NUB + 1))
                nc.scalar.activation(v, v, ACT.Identity, scale=col(outp, 0)
                                     ).then_inc(u_scaled, 1)

            def store_stream(g, u):
                (c, b, q), h = STREAM[u // 2], u % 2
                of = u_before[on_dve[u]]
                act.wait_ge(u_finished if on_dve[u] else u_added, of[NU] * g + of[u] + 1)
                act.dma_start(ov[chan(g, c), b][:, 2 * h:2 * h + 2, BW * q:BW * (q + 1)], ubuf[:, u % NUB, :, :]
                              ).then_inc(u_stored[u % NUB], 16)

            def stage(s, do_a, do_b, do_c, do_next):
                p, ga, gb, gc = plan(do_a, do_b, do_c, on_dve), s, s - 1, s - 2
                for n in range(NT):
                    if do_c:
                        for j in range(NPIECE):
                            if PIECES[j][0] == NT + n:
                                piece(gc, j)
                    if n + 2 < NT:
                        if do_b:
                            split_hi(gb, n + 2)
                    elif do_a:
                        split_hi(ga, n + 2 - NT)
                    if n + AHEAD < NT:
                        if do_b:
                            norm(gb, n + AHEAD)
                    elif do_a:
                        if n + AHEAD == NT:
                            act.wait_ge(gn1_ready, 2 * ga + 2)
                        norm(ga, n + AHEAD - NT)
                    if do_b:
                        for e, w in EDGES:
                            if e == n:
                                copy_edge(gb, e, w)
                        for j in range(NPIECE):
                            if PIECES[j][0] == n:
                                piece(gb, j)
                        for i, at in spill_pos.items():
                            if at == n:
                                spill(gb, i)
                    if do_a and n == STATS1[3]:
                        act.wait_ge(s1_root, s * 2 + 1)
                        nc.scalar.activation(t1[:, 6:7], t1[:, 5:6], ACT.Sqrt).then_inc(s1_root, 1)
                    if do_c:
                        if n == STATS2[2]:
                            act.wait_ge(s2_root, gc * 2 + 1)
                            nc.scalar.activation(t2[:, 6:7], t2[:, 5:6], ACT.Sqrt).then_inc(s2_root, 1)
                            act.wait_ge(gn2_ready, gc + 1)
                        for c in range(CPG):
                            if n == BIAS_SHIFT[c]:
                                act.wait_ge(bias_loaded, 16 * (chan(gc, c) + 1))
                                nc.scalar.activation(bias[:, :], bias[:, :], ACT.Identity, bias=col(outp, 1)
                                                     ).then_inc(bias_shifted, 1)
                        for u in range(NU):
                            if p.u[u] == n and not on_dve[u]:
                                scale_stream(gc, u)
                        for blk in KEPT:
                            if kept_pos[blk][1] + 1 == n:
                                store_kept(gc, blk)
                        for u in range(NU):
                            if p.u_store[u] == n:
                                store_stream(gc, u)

            stages(act, stage)
            for blk in KEPT:
                act.wait_ge(kept_stored[blk], 16 * G)
            for i in range(NUB):
                act.wait_ge(u_stored[i], 16 * G * (NU // NUB))
            for s in x1_spilled.values():
                act.wait_ge(s, 16 * CH)

        @block.vector
        def _(dve):
            nc.vector.memset(zeros, 0.0).then_inc(zeros_ready, 1)
            dve.wait_ge(wall_loaded, 16)
            wv = wall.rearrange("p (c i) -> p c i", c=CH)
            hiw, low = squares[:, 0:CH], squares[:, CH:2 * CH]
            nc.vector.tensor_reduce(out=hiw, in_=wv, axis=AX.X, op=ALU.max).then_inc(scale_chain, 1)
            nc.vector.tensor_reduce(out=low, in_=wv, axis=AX.X, op=ALU.min).then_inc(scale_chain, 1)
            dve.wait_ge(scale_chain, 2)
            nc.vector.scalar_tensor_tensor(out=hiw, in0=low, scalar=-1.0, in1=hiw, op0=ALU.mult,
                                           op1=ALU.max).then_inc(scale_chain, 1)
            dve.wait_ge(scale_chain, 3)
            nc.vector.tensor_scalar(low, hiw, 1e-30, None, ALU.max).then_inc(scale_chain, 1)
            dve.wait_ge(scale_chain, 4)
            nc.vector.tensor_scalar(wsc[:, :, 1], low, 1.0 / WSCALE, None, ALU.mult).then_inc(scale_chain, 1)
            dve.wait_ge(scale_chain, 5)
            nc.vector.reciprocal(wsc[:, :, 0], wsc[:, :, 1]).then_inc(scale_chain, 1)

            def split_lo(g, n):
                N = NT * g + n
                dve.wait_ge(hi_ready, N + 1)
                nc.vector.tensor_tensor(XT[:, n % NB3, 1, :, 2:P + 2], psT[n % NB3][:, :, :],
                                        XT[:, n % NB3, 0, :, 2:P + 2], ALU.subtract).then_inc(lo_ready, 1)

            def evict(g, n):
                c, b, t = TILES[n]
                N = NT * g + n
                c0, c1 = out_columns(b, t)
                y = psY[n % NB3][:, :, c0:c1]
                xs = slot(c, b)[:, :, STEP * t + c0:STEP * t + c1]
                dve.wait_ge(convolved, N + 1)
                if n % NTC == 0:
                    dve.wait_ge(wback_ready, chan(g, c) + 1)
                if is_diag[n]:
                    nc.vector.tensor_tensor(y, y, mask_at(b, t, c0, c1), ALU.mult).then_inc(conv_masked, 1)
                    dve.wait_ge(conv_masked, ND * g + DIAG_BEFORE[n] + 1)
                nc.vector.scalar_tensor_tensor(out=xs, in0=y, scalar=col(wback, c), in1=xs,
                                               op0=ALU.mult, op1=ALU.add, accum_out=sums[:, n:n + 1]
                                               ).then_inc(evicted, 1)

            def take_stats(half, src):
                c, b, q, h = half
                for k in range(2):
                    if q <= b:
                        e = ((c * (NBAND * (NBAND + 1) // 2) + b * (b + 1) // 2 + q) * K) + 2 * h + k
                    else:
                        up = sum(NBAND - 1 - bb for bb in range(b)) + q - b - 1
                        e = LO_ENTRIES + (c * UPPER_PER_CH + up) * K + 2 * h + k
                    last = nc.vector.bn_stats(entries[:, e, :], src[:, k, :])
                return last

            def stream_stats(g, a):
                uses = (NA - a % NAB + NAB - 1) // NAB
                dve.wait_ge(a_loaded[a % NAB], 16 * (g * uses + a // NAB + 1))
                take_stats(A_STREAM[a], abuf[:, a % NAB, :, :]).then_inc(a_done, 1)

            def early_stats(g, i):
                c, b, q, h = A_EARLY[i]
                if h == 0:
                    dve.wait_ge(x_loaded[(c, b, q)], 16 * (chan(g, c) + 1))
                take_stats(A_EARLY[i], transit[b][:, 2 * h:2 * h + 2, BW * q:BW * (q + 1)]).then_inc(early_done, 1)

            def inv_root(v, t, chain, base, root, g):
                dve.wait_ge(root, 2 * g + 2)
                nc.vector.reciprocal(t[:, 7:8], t[:, 6:7]).then_inc(chain, 1)
                dve.wait_ge(chain, base + 1)
                nc.vector.scalar_tensor_tensor(out=t[:, 8:9], in0=t[:, 7:8], scalar=t[:, 5:6], in1=t[:, 6:7],
                                               op0=ALU.mult, op1=ALU.add).then_inc(chain, 1)
                dve.wait_ge(chain, base + 2)
                nc.vector.tensor_scalar(t[:, 8:9], t[:, 8:9], 0.5, None, ALU.mult).then_inc(chain, 1)
                dve.wait_ge(chain, base + 3)
                nc.vector.reciprocal(t[:, 9:10], t[:, 8:9]).then_inc(chain, 1)
                dve.wait_ge(chain, base + 4)

            L1 = 11

            def stats1(g, part):
                base = g * L1
                if part == 0:
                    dve.wait_ge(a_done, NA * (g + 1))
                    dve.wait_ge(early_done, len(A_EARLY) * (g + 1))
                    nc.vector.memset(t1[:, 14:15], 0.0).then_inc(s1_chain, 1)
                    flat_e = entries[:, :, :].rearrange("p e s -> p (e s)")
                    nc.vector.bn_aggr(t1[:, 0:2], flat_e).then_inc(s1_chain, 1)
                    nc.vector.bn_aggr(nxt[:, 1:3], flat_e[:, LO_ENTRIES * 6:]).then_inc(s1_chain, 1)
                elif part == 1:
                    dve.wait_ge(s1_pool, 2 * g + 1)
                    nc.vector.tensor_scalar(col(nxt, 0), t1[:, 2:3], 1.0 / P, None, ALU.mult).then_inc(s1_chain, 1)
                    dve.wait_ge(s1_chain, base + 4)
                    nc.vector.tensor_tensor(t1[:, 10:11], t1[:, 0:1], col(nxt, 0), ALU.subtract
                                            ).then_inc(s1_chain, 1)
                    dve.wait_ge(s1_chain, base + 5)
                    nc.vector.scalar_tensor_tensor(out=t1[:, 3:4], in0=t1[:, 10:11], scalar=t1[:, 10:11],
                                                   in1=t1[:, 1:2], op0=ALU.mult, op1=ALU.add).then_inc(s1_chain, 1)
                elif part == 2:
                    dve.wait_ge(s1_pool, 2 * g + 2)
                    nc.vector.tensor_scalar(t1[:, 5:6], t1[:, 4:5], 1.0 / P, EPS, ALU.mult, ALU.add
                                            ).then_inc(s1_root, 1)
                else:
                    inv_root(g, t1, s1_chain, base + 6, s1_root, g)
                    nc.vector.scalar_tensor_tensor(out=t1[:, 11:12], in0=t1[:, 9:10], scalar=-1.0, in1=col(nxt, 0),
                                                   op0=ALU.mult, op1=ALU.mult).then_inc(s1_chain, 1)
                    dve.wait_ge(s1_chain, base + 11)

            def hand_over_norm(ga, gb):
                if gb is not None:
                    dve.wait_ge(diag_normed, ND * (gb + 1))
                nc.vector.tensor_copy(normp[:, 0:1], t1[:, 9:10]).then_inc(gn1_ready, 1)
                nc.vector.tensor_copy(normp[:, 1:2], t1[:, 11:12]).then_inc(gn1_ready, 1)

            def hand_over_sums(g):
                nc.vector.tensor_copy(cur[:, 0:3], nxt[:, :]).then_inc(cur_ready, 1)
                nc.vector.tensor_scalar(col(cur, 3), col(nxt, 0), -1.0, None, ALU.mult).then_inc(cur_ready, 1)

            NUP = float(CPG * UPPER_PER_CH * K * BW)
            L2 = 13

            def sum_tiles(g):
                dve.wait_ge(evicted, NT * (g + 1))
                nc.vector.tensor_reduce(out=t2[:, 0:1], in_=sums[:, :], axis=AX.X, op=ALU.add).then_inc(tiles_summed, 1)

            def stats2(g, part):
                base = g * L2

                def link(i, ins):
                    ins.then_inc(s2_chain, 1)
                    dve.wait_ge(s2_chain, base + i)
                if part == 0:
                    dve.wait_ge(pieces_done, NPIECE * (g + 1))
                    nc.vector.tensor_reduce(out=t2[:, 1:2], in_=squares[:, :], axis=AX.X, op=ALU.add
                                            ).then_inc(squares_read, 1)
                    link(1, nc.vector.tensor_tensor(t2[:, 10:11], col(cur, 1), col(cur, 0), ALU.subtract))
                    link(2, nc.vector.scalar_tensor_tensor(out=t2[:, 11:12], in0=t2[:, 10:11], scalar=t2[:, 10:11],
                                                           in1=col(cur, 2), op0=ALU.mult, op1=ALU.add))
                    dve.wait_ge(tiles_summed, g + 1)
                    nc.vector.scalar_tensor_tensor(out=t2[:, 0:1], in0=col(cur, 1), scalar=NUP, in1=t2[:, 0:1],
                                                   op0=ALU.mult, op1=ALU.add).then_inc(s2_chain, 1)
                    dve.wait_ge(squares_read, g + 1)
                    nc.vector.scalar_tensor_tensor(out=t2[:, 1:2], in0=t2[:, 11:12], scalar=NUP, in1=t2[:, 1:2],
                                                   op0=ALU.mult, op1=ALU.add).then_inc(s2_chain, 1)
                elif part == 1:
                    dve.wait_ge(s2_pool, g + 1)
                    link(5, nc.vector.tensor_scalar(t2[:, 4:5], t2[:, 2:3], 1.0 / ROWN, None, ALU.mult))
                    link(6, nc.vector.tensor_tensor(t2[:, 14:15], t2[:, 4:5], col(cur, 0), ALU.subtract))
                    link(7, nc.vector.tensor_tensor(t2[:, 12:13], t2[:, 14:15], t2[:, 14:15], ALU.mult))
                    link(8, nc.vector.scalar_tensor_tensor(out=t2[:, 13:14], in0=t2[:, 3:4], scalar=1.0 / ROWN,
                                                           in1=t2[:, 12:13], op0=ALU.mult, op1=ALU.subtract))
                    nc.vector.tensor_scalar(t2[:, 5:6], t2[:, 13:14], 0.0, EPS, ALU.max, ALU.add).then_inc(s2_root, 1)
                else:
                    wait(dve, u_scaled, N_POOL * g)
                    inv_root(g, t2, s2_chain, base + 8, s2_root, g)
                    link(13, nc.vector.tensor_scalar(col(outp, 0), t2[:, 9:10], 1.0, None, ALU.add))
                    nc.vector.scalar_tensor_tensor(out=col(outp, 1), in0=t2[:, 9:10], scalar=-1.0,
                                                   in1=t2[:, 4:5], op0=ALU.mult, op1=ALU.mult).then_inc(gn2_ready, 1)

            def build_weights(g, c):
                sc = wsc[:, bass.ds(chan(g, c), 1), 0]
                dve.wait_ge(w_loaded, 16 * K * (chan(g, c) + 1))
                wait(dve, convolved, NT * g if c else NT * (g - 1) + NTC)
                if isinstance(g, int) and g == 0 and c == 0:
                    dve.wait_ge(scale_chain, 6)
                nc.vector.tensor_copy(col(wback, c), wsc[:, bass.ds(chan(g, c), 1), 1]).then_inc(wback_ready, 1)
                nc.vector.tensor_scalar(wsplit[:, c, 0, :, :], wstage[:, :, :], sc, None, ALU.mult
                                        ).then_inc(w_hi_built, 1)
                dve.wait_ge(w_hi_built, chan(g, c) + 1)
                nc.vector.scalar_tensor_tensor(out=wsplit[:, c, 1, :, :], in0=wstage[:, :, :], scalar=sc,
                                               in1=wsplit[:, c, 0, :, :], op0=ALU.mult, op1=ALU.subtract
                                               ).then_inc(w_built, 1)

            def finish_kept(g, blk, h):
                c, b, q = blk
                if h == 0:
                    dve.wait_ge(bias_shifted, chan(g, c) + 1)
                v = kept[(c, b)][:, 2 * h:2 * h + 2, BW * q:BW * (q + 1)]
                nc.vector.scalar_tensor_tensor(out=v, in0=v, scalar=col(outp, 0), in1=bias_at(b, q, h),
                                               op0=ALU.mult, op1=ALU.add).then_inc(kept_done, 1)

            def finish_stream(g, u):
                (c, b, q), h = STREAM[u // 2], u % 2
                dve.wait_ge(bias_shifted, chan(g, c) + 1)
                dve.wait_ge(u_loaded[u % NUB], 16 * (g * (NU // NUB) + u // NUB + 1))
                v = ubuf[:, u % NUB, :, :]
                nc.vector.scalar_tensor_tensor(out=v, in0=v, scalar=col(outp, 0), in1=bias_at(b, q, h),
                                               op0=ALU.mult, op1=ALU.add).then_inc(u_finished, 1)

            def stage(s, do_a, do_b, do_c, do_next):
                p, ga, gb, gc = plan(do_a, do_b, do_c, on_dve), s, s - 1, s - 2
                for n in range(NT):
                    if n + 2 < NT:
                        if do_b:
                            split_lo(gb, n + 2)
                    elif do_a:
                        split_lo(ga, n + 2 - NT)
                    if n >= 1:
                        if do_b:
                            evict(gb, n - 1)
                    elif do_c:
                        evict(gc, NT - 1)
                    if do_c:
                        if n == 0:
                            sum_tiles(gc)
                        if n in STATS2:
                            stats2(gc, STATS2.index(n))
                        for blk in KEPT:
                            for h in range(2):
                                if kept_pos[blk][h] == n:
                                    finish_kept(gc, blk, h)
                        for u in range(NU):
                            if p.u[u] == n and on_dve[u]:
                                finish_stream(gc, u)
                    for g, a in a_items(p, p.a, s, n, do_next):
                        stream_stats(g, a)
                    if do_a:
                        if n in EARLY_STATS:
                            early_stats(ga, EARLY_STATS.index(n))
                        for part, at in enumerate(STATS1):
                            if at == n:
                                stats1(ga, part)
                        if n == W_BUILD[0]:
                            build_weights(ga, 0)
                        if n == HAND_OVER_NORM:
                            hand_over_norm(ga, gb if do_b else None)
                    if do_b and n == HAND_OVER_SUMS:
                        hand_over_sums(gb)
                    if do_b and n == W_BUILD[1]:
                        build_weights(gb, 1)
            stages(dve, stage)

        @block.gpsimd
        def _(pool):
            nc.gpsimd.iota(pos_in, pattern=[[1, NPOS]], base=-(HH - 1), channel_multiplier=0,
                           allow_small_or_imprecise_dtypes=True).then_inc(pos_ready, 1)
            nc.gpsimd.memset(mask[:, :], 1.0).then_inc(const_ready, 1)
            nc.gpsimd.memset(ident[:, :], 0.0).then_inc(const_ready, 1)
            nc.gpsimd.memset(xn[:, :, :, :, :], 0.0).then_inc(const_ready, 1)
            nc.gpsimd.memset(wstage[:, :, :], 0.0).then_inc(const_ready, 1)
            pool.wait_ge(const_ready, 4)
            nc.gpsimd.affine_select(out=mask[:, :], in_=mask[:, :], pattern=[[1, MW]], compare_op=ALU.is_ge,
                                    fill=0.0, base=MLO, channel_multiplier=K).then_inc(const_ready, 1)
            nc.gpsimd.affine_select(out=ident[:, :], in_=ident[:, :], pattern=[[-1, P]], compare_op=ALU.not_equal,
                                    fill=1.0, base=0, channel_multiplier=1).then_inc(const_ready, 1)
            pool.wait_ge(const_ready, 6)

            def mask_tile(g, n):
                c, b, t = TILES[n]
                pool.wait_ge(diag_normed, ND * g + DIAG_BEFORE[n] + 1)
                v = xn[:, n % NB3, :, :, :]
                m = mask_at(b, t, 0, TIN)
                m = bass.AP(m.tensor, m.offset, [m.ap[0], [-XC, NPC], [1, K], [-1, XC]])
                nc.gpsimd.tensor_tensor(v, v, m, ALU.mult).then_inc(xn_ready, 1)

            def halo_from(g, n):
                c, b, t = TILES[n]
                N = NT * g + n
                if n % NTC == 0:
                    wait_alone(pool, halo_out, N)
                    nc.gpsimd.memset(halo[:, :, :, :, :], 0.0).then_inc(halo_zeroed, 1)
                    wait_alone(pool, halo_zeroed, chan(g, c) + 1)
                wait_alone(pool, convolved, N - NB3 + 1)
                for e, _ in EDGES:
                    if n > e and (c, t) == (TILES[e][0], TILES[e][2] + 1):
                        wait_alone(pool, edge_copied, 16 * K * (NEDGE * g + edges_before(n)))
                nc.gpsimd.tensor_copy(XT[:, n % NB3, :, :, 0:2], halo[:, t, :, :, :]).then_inc(halo_in, 1)

            def halo_to(g, n):
                c, b, t = TILES[n]
                N = NT * g + n
                wait_alone(pool, halo_in, N + 1)
                wait_alone(pool, lo_ready, N + 1)
                nc.gpsimd.tensor_copy(halo[:, t, :, :, :], XT[:, n % NB3, :, :, P:P + 2]).then_inc(halo_out, 1)

            def add_bias(g, u):
                (c, b, q), h = STREAM[u // 2], u % 2
                if u_before[0][u] == u_before[0][c * (NU // CPG)]:
                    wait_alone(pool, bias_shifted, chan(g, c) + 1)
                pool.wait_ge(u_scaled, N_POOL * g + u_before[0][u] + 1)
                v = ubuf[:, u % NUB, :, :]
                nc.gpsimd.tensor_tensor(v, v, bias_at(b, q, h), ALU.add).then_inc(u_added, 1)

            def stage(s, do_a, do_b, do_c, do_next):
                p, ga, gb, gc = plan(do_a, do_b, do_c, on_dve), s, s - 1, s - 2
                for n in range(NT):
                    if n + AHEAD < NT:
                        if do_b and is_diag[n + AHEAD]:
                            mask_tile(gb, n + AHEAD)
                    elif do_a and is_diag[n + AHEAD - NT]:
                        mask_tile(ga, n + AHEAD - NT)
                    if n + 1 < NT:
                        if do_b:
                            halo_to(gb, n + 1)
                    elif do_a:
                        halo_to(ga, 0)
                    if n + 2 < NT:
                        if do_b:
                            halo_from(gb, n + 2)
                    elif do_a:
                        halo_from(ga, n + 2 - NT)
                    if do_a and n == STATS1[0]:
                        wait_alone(pool, s1_chain, 11 * ga + 3)
                        nc.gpsimd.partition_all_reduce(t1[:, 2:3], t1[:, 0:1], P, RED.add).then_inc(s1_pool, 1)
                    if do_a and n == STATS1[1]:
                        wait_alone(pool, s1_chain, 11 * ga + 6)
                        nc.gpsimd.partition_all_reduce(t1[:, 4:5], t1[:, 3:4], P, RED.add).then_inc(s1_pool, 1)
                    if do_c:
                        if n == STATS2[0]:
                            wait_alone(pool, s2_chain, 13 * gc + 4)
                            nc.gpsimd.partition_all_reduce(t2[:, 2:4], t2[:, 0:2], P, RED.add).then_inc(s2_pool, 1)
                        for u in range(NU):
                            if p.u[u] == n and not on_dve[u]:
                                add_bias(gc, u)

            stages(pool, stage)

        @block.tensor
        def _(pe):
            pe.wait_ge(small_loaded, 96)
            pe.wait_ge(h1_ready, 1)
            for j in range(NPOS // BW):
                cols = slice(j * BW, (j + 1) * BW)
                if j >= 2:
                    pe.wait_ge(h2_ready, j - 1)
                nc.tensor.matmul(psT[j % 2][0:DIM, :, :].rearrange("p a b -> p (a b)"), w2s[:, :], h1[:, cols],
                                 start=True, stop=True).then_inc(mlp2_done, 1)
                pe.wait_ge(h2_ready, j + 1)
                if j >= 2:
                    pe.wait_ge(table_ready, j - 1)
                nc.tensor.matmul(psY[j % 2][0:CH, :, :].rearrange("p a b -> p (a b)"), w3s[:, :], h2[:, cols],
                                 start=True, stop=True).then_inc(mlp3_done, 1)
            pe.wait_ge(table_ready, 8)
            pe.wait_ge(const_ready, 6)

            def transpose(N, m):
                wait(pe, lo_ready, N - NB3 + 1)
                pe.wait_ge(xn_ready, N + 1)
                for i in range(NPC):
                    last = nc.tensor.transpose(psT[m][:, i, :], xn[:, m, i, :, :].rearrange("p k c -> p (k c)"), ident[:, :])
                last.then_inc(transposed, 1)

            def convolve(N, m, c):
                pe.wait_ge(lo_ready, N + 1)
                pe.wait_ge(halo_in, N + 1)
                wait(pe, evicted, N - NB3 + 1)
                products = [(i, sh, xp, wp) for i in range(NPC) for sh in range(3)
                            for xp, wp in ((0, 0), (0, 1), (1, 0))]
                for j, (i, sh, xp, wp) in enumerate(products):
                    lo_c = max(0, PADC - XC * i)
                    hi_c = min(WC, TOUT + PADC - XC * i)
                    rows = min(K, NE - K * sh)
                    o = XC * i - PADC
                    last = nc.tensor.matmul(psY[m][:, 0:rows, o + lo_c:o + hi_c],
                                            XT[:, m, xp, i, 2 - sh:2 - sh + P],
                                            wsplit[:, c, wp, K * sh:K * sh + rows, lo_c:hi_c],
                                            start=(j == 0), stop=(j == len(products) - 1), skip_group_check=True)
                last.then_inc(convolved, 1)

            def triple(N, c, ahead=NB3):
                for i in range(NB3):
                    if i < ahead:
                        transpose(N + i + 2, (i + 2) % NB3)
                    convolve(N + i, i, c)

            def group(g):
                first = NT * g
                pe.wait_ge(w_built, chan(g, 0) + 1)
                triple(first, 0)
                with pe.Fori(1, NTC // NB3) as j:
                    triple(first + NB3 * j, 0)
                pe.wait_ge(w_built, chan(g, 1) + 1)
                triple(first + NTC, 1)
                with pe.Fori(NTC // NB3 + 1, 2 * NTC // NB3 - 1) as j:
                    triple(first + NB3 * j, 1)

            transpose(0, 0)
            transpose(1, 1)
            group(0)
            with pe.Fori(1, G) as g:
                triple(NT * g - NB3, 1)
                group(g)
            triple(NT * G - NB3, 1, 1)


_INS = ["x", "w", "w1", "b1", "w2", "b2", "w3", "b3"]


def kernel(x, L0_conv_weight, L1_conv_W1, L1_conv_b1, L1_conv_W2, L1_conv_b2, L1_conv_W3, L1_conv_b3):
    import numpy as _np
    import concourse.bacc as _bacc
    from concourse import mybir as _mybir
    from concourse.bass_utils import run_bass_kernel_spmd as _run

    nc = _bacc.Bacc("TRN2", target_bir_lowering=False, num_devices=1)
    values = [x, _np.asarray(L0_conv_weight)[:, ::-1, ::-1], L1_conv_W1, L1_conv_b1, L1_conv_W2, L1_conv_b2,
              L1_conv_W3, L1_conv_b3]
    arrays, args = {}, []
    for name, v in zip(_INS, values):
        a = _np.ascontiguousarray(v)
        arrays[f"in_{name}"] = a
        args.append(nc.dram_tensor(f"in_{name}", a.shape, _mybir.dt.from_np(a.dtype), kind="ExternalInput").ap())
    out = nc.dram_tensor("out_0", x.shape, _mybir.dt.float32, kind="ExternalOutput").ap()
    preact_conv_kernel(nc, *args, out)
    r = _run(nc, [arrays], core_ids=[0])
    return r.results[0]["out_0"]
```
